# Optimizing a Trainium2 kernel written in Bass

```python
import numpy as np
import jax
import jax.numpy as jnp

def _softmax(x, axis=-1):
    return jax.nn.softmax(x, axis=axis)

def _gelu(x):
    return jax.nn.gelu(x, approximate=True)

def _silu(x):
    return jax.nn.silu(x)

def _sigmoid(x):
    return jax.nn.sigmoid(x)

def _layernorm(x, axis=-1, eps=1e-05):
    m = jnp.mean(x, axis=axis, keepdims=True)
    v = jnp.var(x, axis=axis, keepdims=True)
    return (x - m) / jnp.sqrt(v + eps)

def _scatter_add(tgt, idx, src, axis=0):
    return tgt.at[idx].add(src)

def _segment_sum(src, seg, n):
    return jax.ops.segment_sum(src, seg, n)
kernel_name = 'mk_cond_seq_d2_seqx_r2_d04e05'

def setup_inputs(seed: int=0):
    np.random.seed(seed)
    _w = jnp.asarray

    def _rec_inputs():
        import jax
        import jax.numpy as jnp
        _rk = jax.random.key(seed)
        x = -0.0005207 + 1.001 * jax.random.normal(jax.random.fold_in(_rk, 1), (2, 2048, 512), jnp.float32)
        _lenS = 2048 - jax.random.randint(jax.random.fold_in(_rk, 7), (2,), 0, max(1, 2048 // 4) + 1, jnp.int32)
        _lenS2 = 2048 - jax.random.randint(jax.random.fold_in(_rk, 8), (2,), 0, max(1, 2048 // 4) + 1, jnp.int32)
        itok_B_34_63 = jax.random.randint(jax.random.fold_in(_rk, 12), (2,), 34, 64, jnp.int32)
        fside_Bx16xSxS_0 = -1.47943e-05 + 1.00017 * jax.random.normal(jax.random.fold_in(_rk, 13), (2, 16, 2048, 2048), jnp.float32)
        condB_theta = jax.random.uniform(jax.random.fold_in(_rk, 14), (2,), jnp.float32, 0.0, 0.983423)
        condB_phi = jax.random.uniform(jax.random.fold_in(_rk, 15), (2,), jnp.float32, 0.0, 0.961312)
        _validS = jnp.arange(2048)[None, :] < _lenS[:, None]
        _validS2 = jnp.arange(2048)[None, :] < _lenS2[:, None]
        _causal = jnp.tril(jnp.ones((2048, 2048), dtype=bool))
        mask_Bx1xSxS_bk0 = jnp.logical_not(jnp.broadcast_to(_validS[:, None, None, :], (2, 1, 2048, 2048)))
        return (x, itok_B_34_63, fside_Bx16xSxS_0, condB_theta, condB_phi, mask_Bx1xSxS_bk0)
    x, itok_B_34_63, fside_Bx16xSxS_0, condB_theta, condB_phi, mask_Bx1xSxS_bk0 = _rec_inputs()

    def _L0_cond_setup():
        import jax, jax.numpy as jnp
        import numpy as np
        import math
        D_MODEL = 512
        N_HEAD = 16
        HEAD_DIM = D_MODEL // N_HEAD
        D_FF = 2048
        NUM_STEPS = 100.0
        RESCALE = 4000.0
        EPS = 1e-05

        def _sin_emb(t):
            half = D_MODEL // 2
            x = t.astype(jnp.float32) / NUM_STEPS * RESCALE
            freqs = jnp.exp(jnp.arange(half, dtype=jnp.float32) * (-math.log(10000.0) / (half - 1)))
            e = x[:, None] * freqs[None, :]
            return jnp.concatenate([jnp.sin(e), jnp.cos(e)], axis=-1)

        def _ln(x):
            m = jnp.mean(x, axis=-1, keepdims=True)
            v = jnp.var(x, axis=-1, keepdims=True)
            return (x - m) / jnp.sqrt(v + EPS)

        def _gelu2(x):
            return x * jax.nn.sigmoid(1.702 * x)
        key = jax.random.key(seed)
        ks = jax.random.split(key, 24)
        B, S, D, F = (4, 256, D_MODEL, D_FF)
        std = 0.02
        inp = {'src': jax.random.normal(ks[0], (B, S, D), dtype=jnp.float32), 'src_mask': jax.random.randint(ks[1], (B, 1, S, S), 0, 2).astype(bool), 'timestep': jax.random.randint(ks[2], (B,), 0, 100, dtype=jnp.int32), 'attention_bias': jax.random.normal(ks[3], (B, N_HEAD, S, S), dtype=jnp.float32), 'W_ada': jax.random.normal(ks[4], (D, 2 * D), dtype=jnp.float32) * std, 'b_ada': jnp.zeros((2 * D,), dtype=jnp.float32), 'Wq': jax.random.normal(ks[5], (D, D), dtype=jnp.float32) * std, 'bq': jnp.zeros((D,), dtype=jnp.float32), 'Wk': jax.random.normal(ks[6], (D, D), dtype=jnp.float32) * std, 'bk': jnp.zeros((D,), dtype=jnp.float32), 'Wv': jax.random.normal(ks[7], (D, D), dtype=jnp.float32) * std, 'bv': jnp.zeros((D,), dtype=jnp.float32), 'Wo': jax.random.normal(ks[8], (D, D), dtype=jnp.float32) * std, 'bo': jnp.zeros((D,), dtype=jnp.float32), 'W1': jax.random.normal(ks[9], (D, F), dtype=jnp.float32) * std, 'b1': jnp.zeros((F,), dtype=jnp.float32), 'W2': jax.random.normal(ks[10], (F, D), dtype=jnp.float32) * std, 'b2': jnp.zeros((D,), dtype=jnp.float32), 'g2': jnp.ones((D,), dtype=jnp.float32), 'beta2': jnp.zeros((D,), dtype=jnp.float32)}
        return inp
    _L0_cond_all = _L0_cond_setup()
    _L0_cond_in = {k: v for k, v in _L0_cond_all.items() if k in ('W_ada', 'b_ada', 'Wq', 'bq', 'Wk', 'bk', 'Wv', 'bv', 'Wo', 'bo', 'W1', 'b1', 'W2', 'b2', 'g2', 'beta2')}
    del _L0_cond_all

    def _L1_cond_setup():
        import jax, jax.numpy as jnp
        import numpy as np
        key = jax.random.key(seed)
        k1, k2, k3 = jax.random.split(key, 3)
        B, N, D = (16, 2048, 512)
        embeddings = jax.random.normal(k1, (B, N, D), dtype=jnp.float32)
        theta = jax.random.uniform(k2, (B,), dtype=jnp.float32)
        phi = jax.random.uniform(k3, (B,), dtype=jnp.float32)
        return {'embeddings': embeddings, 'theta': theta, 'phi': phi}
    _L1_cond_all = _L1_cond_setup()
    _L1_cond_in = {k: v for k, v in _L1_cond_all.items() if k in ()}
    del _L1_cond_all
    return {'x': x, 'itok_B_34_63': itok_B_34_63, 'fside_Bx16xSxS_0': fside_Bx16xSxS_0, 'condB_theta': condB_theta, 'condB_phi': condB_phi, 'mask_Bx1xSxS_bk0': mask_Bx1xSxS_bk0, 'L0_cond_W_ada': _L0_cond_in['W_ada'], 'L0_cond_b_ada': _L0_cond_in['b_ada'], 'L0_cond_Wq': _L0_cond_in['Wq'], 'L0_cond_bq': _L0_cond_in['bq'], 'L0_cond_Wk': _L0_cond_in['Wk'], 'L0_cond_bk': _L0_cond_in['bk'], 'L0_cond_Wv': _L0_cond_in['Wv'], 'L0_cond_bv': _L0_cond_in['bv'], 'L0_cond_Wo': _L0_cond_in['Wo'], 'L0_cond_bo': _L0_cond_in['bo'], 'L0_cond_W1': _L0_cond_in['W1'], 'L0_cond_b1': _L0_cond_in['b1'], 'L0_cond_W2': _L0_cond_in['W2'], 'L0_cond_b2': _L0_cond_in['b2'], 'L0_cond_g2': _L0_cond_in['g2'], 'L0_cond_beta2': _L0_cond_in['beta2']}

def reference(x, itok_B_34_63, fside_Bx16xSxS_0, condB_theta, condB_phi, mask_Bx1xSxS_bk0, L0_cond_W_ada, L0_cond_b_ada, L0_cond_Wq, L0_cond_bq, L0_cond_Wk, L0_cond_bk, L0_cond_Wv, L0_cond_bv, L0_cond_Wo, L0_cond_bo, L0_cond_W1, L0_cond_b1, L0_cond_W2, L0_cond_b2, L0_cond_g2, L0_cond_beta2):
    import jax
    import jax.numpy as jnp

    def _L0_cond_ref(src, src_mask, timestep, attention_bias, W_ada, b_ada, Wq, bq, Wk, bk, Wv, bv, Wo, bo, W1, b1, W2, b2, g2, beta2):
        import jax, jax.numpy as jnp
        import numpy as np
        import math
        D_MODEL = 512
        N_HEAD = 16
        HEAD_DIM = D_MODEL // N_HEAD
        D_FF = 2048
        NUM_STEPS = 100.0
        RESCALE = 4000.0
        EPS = 1e-05

        def _sin_emb(t):
            half = D_MODEL // 2
            x = t.astype(jnp.float32) / NUM_STEPS * RESCALE
            freqs = jnp.exp(jnp.arange(half, dtype=jnp.float32) * (-math.log(10000.0) / (half - 1)))
            e = x[:, None] * freqs[None, :]
            return jnp.concatenate([jnp.sin(e), jnp.cos(e)], axis=-1)

        def _ln(x):
            m = jnp.mean(x, axis=-1, keepdims=True)
            v = jnp.var(x, axis=-1, keepdims=True)
            return (x - m) / jnp.sqrt(v + EPS)

        def _gelu2(x):
            return x * jax.nn.sigmoid(1.702 * x)
        B, S, D = src.shape
        emb = jax.nn.silu(_sin_emb(timestep)) @ W_ada + b_ada
        scale, shift = jnp.split(emb[:, None, :], 2, axis=-1)
        x = _ln(src) * (1.0 + scale) + shift
        q = (x @ Wq + bq).reshape(B, S, N_HEAD, HEAD_DIM).transpose(0, 2, 1, 3)
        k = (x @ Wk + bk).reshape(B, S, N_HEAD, HEAD_DIM).transpose(0, 2, 1, 3)
        v = (x @ Wv + bv).reshape(B, S, N_HEAD, HEAD_DIM).transpose(0, 2, 1, 3)
        scores = jnp.einsum('bhqd,bhkd->bhqk', q / math.sqrt(HEAD_DIM), k)
        scores = scores + attention_bias
        scores = jnp.where(src_mask, -jnp.inf, scores.astype(jnp.float32))
        probs = jax.nn.softmax(scores, axis=-1).astype(v.dtype)
        ctx = jnp.einsum('bhqk,bhkd->bhqd', probs, v)
        ctx = ctx.transpose(0, 2, 1, 3).reshape(B, S, D)
        x = x + (ctx @ Wo + bo)
        h = _ln(x) * g2 + beta2
        ff = _gelu2(h @ W1 + b1) @ W2 + b2
        return x + ff

    def _L1_cond_ref(embeddings, theta, phi):
        import jax, jax.numpy as jnp
        import numpy as np
        B, N, D = embeddings.shape
        e = embeddings.reshape(B, N, D // 4, 4)
        ct = jnp.cos(theta)[:, None, None]
        st = jnp.sin(theta)[:, None, None]
        cp = jnp.cos(phi)[:, None, None]
        sp = jnp.sin(phi)[:, None, None]
        x0, x1, x2, x3 = (e[..., 0], e[..., 1], e[..., 2], e[..., 3])
        out = jnp.stack([x0 * ct + x1 * st, -x0 * st + x1 * ct, x2 * cp + x3 * sp, -x2 * sp + x3 * cp], axis=-1)
        return out.reshape(B, N, D)
    x = _L0_cond_ref(x, mask_Bx1xSxS_bk0, itok_B_34_63, fside_Bx16xSxS_0, L0_cond_W_ada, L0_cond_b_ada, L0_cond_Wq, L0_cond_bq, L0_cond_Wk, L0_cond_bk, L0_cond_Wv, L0_cond_bv, L0_cond_Wo, L0_cond_bo, L0_cond_W1, L0_cond_b1, L0_cond_W2, L0_cond_b2, L0_cond_g2, L0_cond_beta2)
    x = _L1_cond_ref(x, condB_theta, condB_phi)
    return x

_drawn_inputs = setup_inputs


def setup_inputs(seed=0):
    import zlib

    import numpy as np

    out = dict(_drawn_inputs(seed))
    spreads = {'L0_cond_b_ada': (0.0, 0.1),
     'L0_cond_bq': (0.0, 0.8),
     'L0_cond_bk': (0.0, 0.8),
     'L0_cond_bv': (0.0, 0.1),
     'L0_cond_bo': (0.0, 0.1),
     'L0_cond_b1': (0.0, 0.1),
     'L0_cond_b2': (0.0, 0.1),
     'L0_cond_g2': (1.0, 0.2),
     'L0_cond_beta2': (0.0, 0.358)}
    factors = {'fside_Bx16xSxS_0': 8.0, 'L0_cond_Wq': 8.0, 'L0_cond_Wk': 8.0}
    for name, (base, spread) in spreads.items():
        noise = np.random.default_rng([zlib.crc32(name.encode()), seed]).standard_normal(out[name].shape)
        drawn = base * np.exp(spread * noise) if base else spread * noise
        out[name] = jnp.asarray(drawn.astype(out[name].dtype))
    for name, factor in factors.items():
        out[name] = (out[name] * factor).astype(out[name].dtype)
    return out
```

```python
import math
from contextlib import ExitStack

import numpy as np

import concourse.bass as bass
from concourse import mybir

F32 = mybir.dt.float32
F32R = mybir.dt.float32r
BF16 = mybir.dt.bfloat16
U8 = mybir.dt.uint8
I32 = mybir.dt.int32
ALU = mybir.AluOpType
ACT = mybir.ActivationFunctionType
AXIS_X = mybir.AxisListType.X

P = 128
B, S, D, F = 2, 2048, 512, 2048
H = 16
DH = D // H
DB = D // P
FB = F // P
TOK = 512
QT = TOK // P
NS = S // TOK
NU = B * NS
KB = S // P
EPS = 1e-5
MASKED = -3.0e38
QSCALE = 1.0 / math.sqrt(DH)
NUM_STEPS, RESCALE = 100.0, 4000.0

TWO_PI_1 = 6.28125
TWO_PI_2 = float(np.float32(math.floor((2 * math.pi - TWO_PI_1) * 2**21) / 2**21))
TWO_PI_3 = 2 * math.pi - TWO_PI_1 - TWO_PI_2
ROUNDER = 1.5 * 2.0**23
SIN_MAX = 3.1415925


def chain(eng, sem, base):
    count = [0]

    def link(ins):
        count[0] += 1
        ins.then_inc(sem, 1)
        eng.wait_ge(sem, base + count[0])

    link.count = count
    return link


def phase_a(nc, sem, x, timestep, mask, theta, phi, W_ada, b_ada, Wq, bq, Wk, bk, Wv, bv, freqs,
            q_parts, k_parts, v_heads, xm_scratch, pen_scratch, ident, sel4, trig):
    with ExitStack() as ctx:
        def sb(name, shape, dt=F32):
            return ctx.enter_context(nc.sbuf_tensor(name, shape, dt))

        freq = sb("freq", [P, 2])
        t_int = sb("t_int", [P, B], I32)
        t_f32 = sb("t_f32", [P, B])
        angle = sb("angle", [P, 16])
        quarter = sb("quarter", [P, 16])
        turns = sb("turns", [P, 16])
        emb_sig = sb("emb_sig", [P, 8])
        emb_act = sb("emb_act", [P, 8])
        emb_wide = sb("emb_wide", [P, 8, P])
        w_ada = sb("w_ada", [P, DB, 2 * D])
        b_ada_all = sb("b_ada_all", [P, 2 * D])
        scale1 = sb("scale1", [P, B, D])
        shift = sb("shift", [P, B, D])
        wk = sb("wk", [P, DB, D])
        wq = sb("wq", [P, DB, D])
        wv = sb("wv", [P, DB, D])
        bq_col = sb("bq_col", [P, DB])
        bk_col = sb("bk_col", [P, DB])
        bv_all = sb("bv_all", [P, D])
        eps_a = sb("eps_a", [P, 1])
        xin = sb("xin", [P, QT, D])
        stats = sb("stats", [P, QT, 6])
        mean_var = sb("mean_var", [P, QT, 2])
        std = sb("std", [P, QT])
        rstd = sb("rstd", [P, QT])
        xm = sb("xm", [P, QT, D])
        xT = sb("xT", [P, DB, TOK])
        mask_in = sb("mask_in", [P, QT, S], U8)
        pen = sb("pen", [P, QT, S], BF16)
        exact = sb("exact", [P, 2, TOK])
        part_hi = sb("part_hi", [P, 4, TOK], F32R)
        part_lo = sb("part_lo", [P, 4, TOK], F32R)
        v_out = sb("v_out", [P, 4, D])
        bankT = [ctx.enter_context(nc.psum_tensor(f"a_T{i}", [P, TOK], F32)) for i in range(4)]
        bankG = [ctx.enter_context(nc.psum_tensor(f"a_G{i}", [P, TOK], F32)) for i in range(4)]

        const_ready = sem("const_ready")
        small_in = sem("small_in")
        w_ada_in = sem("w_ada_in")
        w_in = sem("w_in")
        a_chain = sem("a_chain")
        angles_ready = sem("angles_ready")
        sines_ready = sem("sines_ready")
        emb_ready = sem("emb_ready")
        ada_ready = sem("ada_ready")
        ada_used = sem("ada_used")
        x_in = sem("x_in")
        x_used = sem("x_used")
        var_ready = sem("var_ready")
        std_ready = sem("std_ready")
        ln_chain = sem("ln_chain")
        xm_ready = sem("xm_ready")
        xm_stored = sem("xm_stored")
        xt_psum = sem("xt_psum")
        xt_ready = sem("xt_ready")
        proj_ready = sem("proj_ready")
        proj_used = sem("proj_used")
        part_chain = sem("part_chain")
        staged = sem("staged")
        stored = [sem(f"stored{i}") for i in range(4)]
        mask_ld = sem("mask_ld")
        pen_ready = sem("pen_ready")
        pen_stored = sem("pen_stored")

        NG = 3 * DB
        STORES = 2 * 32 + 16

        block = ctx.enter_context(nc.Block())

        @block.gpsimd
        def _(pool):
            nc.gpsimd.memset(ident[:], 0.0).then_inc(const_ready, 1)
            nc.gpsimd.memset(sel4[:], 0.0).then_inc(const_ready, 1)
            pool.wait_ge(const_ready, 2)
            nc.gpsimd.affine_select(out=ident[:], in_=ident[:], compare_op=ALU.not_equal, fill=1.0,
                                    base=0, pattern=[[-1, P]], channel_multiplier=1).then_inc(const_ready, 1)
            for j in range(4):
                pool.wait_ge(const_ready, 3 + j)
                nc.gpsimd.affine_select(out=sel4[:], in_=sel4[:], compare_op=ALU.not_equal, fill=1.0,
                                        base=-DH * j, pattern=[[-1, DH]], channel_multiplier=1).then_inc(const_ready, 1)

        @block.sync
        def _(sp):
            sp.dma_start(freq[:], freqs.rearrange("(c p) -> p c", p=P), allow_slow_non_contiguous=True).then_inc(small_in, 16)
            sp.dma_start(t_int[:], timestep.rearrange("(o b) -> o b", o=1).to_broadcast([P, B])).then_inc(small_in, 16)
            for b in range(B):
                for c in (8 + b, 12 + b):
                    sp.dma_start(angle[:, c:c + 1], theta[b:b + 1].rearrange("(o b) -> o b", o=1).to_broadcast([P, 1]), allow_slow_non_contiguous=True).then_inc(small_in, 16)
                for c in (10 + b, 14 + b):
                    sp.dma_start(angle[:, c:c + 1], phi[b:b + 1].rearrange("(o b) -> o b", o=1).to_broadcast([P, 1]), allow_slow_non_contiguous=True).then_inc(small_in, 16)
            sp.dma_start(b_ada_all[:], b_ada.rearrange("(o n) -> o n", o=1).to_broadcast([P, 2 * D])).then_inc(small_in, 16)
            sp.dma_start(bq_col[:], bq.rearrange("(c p) -> p c", p=P), allow_slow_non_contiguous=True).then_inc(small_in, 16)
            sp.dma_start(bk_col[:], bk.rearrange("(c p) -> p c", p=P), allow_slow_non_contiguous=True).then_inc(small_in, 16)
            sp.dma_start(bv_all[:], bv.rearrange("(o n) -> o n", o=1).to_broadcast([P, D])).then_inc(small_in, 16)
            sp.dma_start(w_ada[:], W_ada.rearrange("(c p) n -> p c n", p=P)).then_inc(w_ada_in, 16)
            sp.dma_start(wk[:], Wk.rearrange("(c p) n -> p c n", p=P)).then_inc(w_in, 16)
            sp.dma_start(wq[:], Wq.rearrange("(c p) n -> p c n", p=P)).then_inc(w_in, 16)
            sp.dma_start(wv[:], Wv.rearrange("(c p) n -> p c n", p=P)).then_inc(w_in, 16)
            sp.sem_inc(xm_stored, 16)
            sp.sem_inc(pen_stored, 16)
            for i in range(4):
                sp.sem_inc(stored[i], 16)
            with sp.Fori(0, B) as b:
                with sp.Fori(0, NS) as s:
                    u = b * NS + s
                    sp.wait_ge(xm_ready, u + 1)
                    sp.dma_start(xm_scratch[bass.ds(u, 1)].rearrange("u p n -> (u p) n"),
                                 xm[:].rearrange("p t n -> p (t n)")).then_inc(xm_stored, 16)
                    for g in range(NG):
                        if g == 6:
                            sp.wait_ge(pen_ready, u * QT + QT)
                            sp.dma_start(pen_scratch[bass.ds(u, 1)].rearrange("u p n -> (u p) n"),
                                         pen[:].rearrange("p t n -> p (t n)")).then_inc(pen_stored, 16)
                        if g < 2 * DB:
                            sp.wait_ge(staged, u * 2 * DB + g + 1)
                        else:
                            sp.wait_ge(proj_used, u * NG + g + 5)
                        i = g % 4
                        if g < 2 * DB:
                            to = k_parts if g < DB else q_parts
                            for n, part in enumerate((part_hi, part_lo)):
                                sp.dma_start(to[bass.ds(b * 2 + n, 1), i * P:(i + 1) * P, bass.ds(s * TOK, TOK)].rearrange("o r n -> (o r) n"),
                                             part[:, i, :].bitcast(F32)).then_inc(stored[i], 16)
                        else:
                            sp.dma_start(v_heads[bass.ds(b, 1), :, :, bass.ds((s * QT + i) * DH, DH)].rearrange("o h p d -> p (o h) d"),
                                         v_out[:, i, :].rearrange("p (h d) -> p h d", h=H)).then_inc(stored[i], 16)
            for i in range(4):
                sp.wait_ge(stored[i], 16 + NU * STORES)
            sp.wait_ge(xm_stored, 16 + NU * 16)
            sp.wait_ge(pen_stored, 16 + NU * 16)

        @block.scalar
        def _(act):
            act.wait_ge(angles_ready, 1)
            nc.scalar.activation(trig[:], angle[:], ACT.Sin).then_inc(sines_ready, 1)
            act.wait_ge(sines_ready, 1)
            nc.scalar.activation(emb_sig[:], trig[:, 0:8], ACT.Sigmoid).then_inc(sines_ready, 1)
            act.sem_inc(xt_ready, 4)
            with act.Fori(0, NU) as u:
                act.wait_ge(x_used, u + 1)
                act.dma_start(xin[:].rearrange("p t n -> p t n"),
                              x[bass.ds(u, 1)].rearrange("u (t p) n -> p (u t) n", p=P)).then_inc(x_in, 16)
                act.dma_start(mask_in[:], mask[bass.ds(u, 1)].rearrange("u (t p) n -> p (u t) n", p=P)).then_inc(mask_ld, 16)
                act.wait_ge(var_ready, u + 1)
                nc.scalar.activation(std[:], mean_var[:, :, 1], ACT.Sqrt, bias=eps_a[:]).then_inc(std_ready, 1)
                act.wait_ge(mask_ld, u * 16 + 16)
                act.wait_ge(pen_stored, u * 16 + 16)
                for t in range(QT):
                    nc.scalar.activation(pen[:, t, :], mask_in[:, t, :], ACT.Copy, scale=MASKED).then_inc(pen_ready, 1)
                act.wait_ge(pen_ready, u * QT + QT)
                for c in range(DB):
                    act.wait_ge(xt_psum, u * DB + c + 1 + 4)
                    act.wait_ge(proj_ready, u * NG + 12)
                    nc.scalar.copy(xT[:, c, :], bankT[c][:]).then_inc(xt_ready, 1)

        @block.vector
        def _(dve):
            link = chain(dve, a_chain, 0)
            nc.vector.memset(eps_a[:], EPS)
            nc.vector.memset(quarter[:, 0:4], 0.0)
            nc.vector.memset(quarter[:, 4:8], 0.25)
            nc.vector.memset(quarter[:, 8:12], 0.0)
            link(nc.vector.memset(quarter[:, 12:16], 0.25))
            dve.wait_ge(small_in, 14 * 16)
            link(nc.vector.tensor_copy(t_f32[:], t_int[:]))
            link(nc.vector.tensor_scalar(t_f32[:], t_f32[:], RESCALE / NUM_STEPS, None, ALU.mult))
            for k in range(2):
                for c in range(2):
                    last = nc.vector.tensor_scalar(angle[:, 4 * k + 2 * c:4 * k + 2 * c + 2], t_f32[:], freq[:, c:c + 1], None, ALU.mult)
            link(last)
            link(nc.vector.scalar_tensor_tensor(out=turns[:], in0=angle[:], scalar=1.0 / (2 * math.pi),
                                                in1=quarter[:], op0=ALU.mult, op1=ALU.add))
            link(nc.vector.tensor_scalar(turns[:], turns[:], ROUNDER, ROUNDER, ALU.add, ALU.subtract))
            for part in (TWO_PI_1, TWO_PI_2, TWO_PI_3):
                link(nc.vector.scalar_tensor_tensor(out=angle[:], in0=turns[:], scalar=-part,
                                                    in1=angle[:], op0=ALU.mult, op1=ALU.add))
            link(nc.vector.scalar_tensor_tensor(out=angle[:], in0=quarter[:], scalar=2 * math.pi,
                                                in1=angle[:], op0=ALU.mult, op1=ALU.add))
            nc.vector.tensor_scalar(angle[:], angle[:], SIN_MAX, -SIN_MAX, ALU.min, ALU.max).then_inc(angles_ready, 1)
            dve.wait_ge(sines_ready, 2)
            link(nc.vector.tensor_tensor(emb_act[:], trig[:, 0:8], emb_sig[:], ALU.mult))
            nc.vector.tensor_copy(emb_wide[:], emb_act[:].rearrange("p (c o) -> p c o", o=1).to_broadcast([P, 8, P])).then_inc(emb_ready, 1)
            for b in range(B):
                dve.wait_ge(ada_ready, 2 * b + 1)
                nc.vector.scalar_tensor_tensor(out=scale1[:, b, :], in0=bankG[2 * b][:], scalar=1.0,
                                               in1=b_ada_all[:, 0:D], op0=ALU.add, op1=ALU.add).then_inc(ada_used, 1)
                dve.wait_ge(ada_ready, 2 * b + 2)
                nc.vector.tensor_tensor(shift[:, b, :], bankG[2 * b + 1][:], b_ada_all[:, D:2 * D], ALU.add).then_inc(ada_used, 1)
            dve.sem_inc(x_used, 1)
            dve.sem_inc(proj_used, 4)
            dve.wait_ge(ada_used, 4)
            LN_LINKS, PART_LINKS = 3, 2 * DB
            with dve.Fori(0, B) as b:
                with dve.Fori(0, NS) as s:
                    u = b * NS + s
                    link = chain(dve, ln_chain, u * LN_LINKS)
                    dve.wait_ge(x_in, u * 16 + 16)
                    for t in range(QT):
                        last = nc.vector.bn_stats(stats[:, t, :], xin[:, t, :])
                    link(last)
                    dve.nop(nofuse=True)
                    for t in range(QT):
                        last = nc.vector.bn_aggr(mean_var[:, t, :], stats[:, t, :])
                    last.then_inc(var_ready, 1)
                    dve.wait_ge(std_ready, u + 1)
                    link(nc.vector.reciprocal(rstd[:], std[:]))
                    dve.wait_ge(xt_psum, u * DB + 4)
                    dve.wait_ge(xm_stored, u * 16 + 16)
                    for t in range(QT):
                        last = nc.vector.tensor_scalar(xm[:, t, :], xin[:, t, :], mean_var[:, t, 0:1], rstd[:, t:t + 1], ALU.subtract, ALU.mult)
                    last.then_inc(x_used, 1)
                    dve.wait_ge(x_used, u + 2)
                    for t in range(QT):
                        last = nc.vector.tensor_tensor(xm[:, t, :], xm[:, t, :], scale1[:, bass.ds(b, 1), :].rearrange("p o n -> p (o n)"), ALU.mult)
                    link(last)
                    for t in range(QT):
                        last = nc.vector.tensor_tensor(xm[:, t, :], xm[:, t, :], shift[:, bass.ds(b, 1), :].rearrange("p o n -> p (o n)"), ALU.add)
                    last.then_inc(xm_ready, 1)
                    assert link.count[0] == LN_LINKS
                    link = chain(dve, part_chain, u * PART_LINKS)
                    for g in range(NG):
                        i = g % 4
                        dve.wait_ge(proj_ready, u * NG + g + 1 + 12)
                        dve.wait_ge(stored[i], u * STORES + 32 * (g // 4) + 16)
                        if g < 2 * DB:
                            bias, scale = (bk_col, 1.0) if g < DB else (bq_col, QSCALE)
                            nc.vector.tensor_scalar(exact[:, g % 2, :], bankG[i][:], bias[:, i:i + 1], scale, ALU.add, ALU.mult).then_inc(proj_used, 1)
                            dve.wait_ge(proj_used, u * NG + g + 5)
                            link(nc.vector.tensor_copy(part_hi[:, i, :], exact[:, g % 2, :]))
                            nc.vector.tensor_tensor(part_lo[:, i, :], exact[:, g % 2, :], part_hi[:, i, :].bitcast(F32), ALU.subtract).then_inc(staged, 1)
                        else:
                            nc.vector.tensor_tensor(v_out[:, i, :], bankG[i][:], bv_all[:], ALU.add).then_inc(proj_used, 1)

        @block.tensor
        def _(pe):
            pe.wait_ge(emb_ready, 1)
            pe.wait_ge(w_ada_in, 16)
            for b in range(B):
                for half in range(2):
                    for c in range(DB):
                        last = nc.tensor.matmul(bankG[2 * b + half][:], emb_wide[:, 2 * c + b, :],
                                                w_ada[:, c, half * D:(half + 1) * D], start=(c == 0), stop=(c == DB - 1))
                    last.then_inc(ada_ready, 1)
            pe.sem_inc(xt_psum, 4)
            pe.sem_inc(proj_ready, 12)
            pe.wait_ge(const_ready, 7)
            pe.wait_ge(ada_used, 4)
            pe.wait_ge(w_in, 48)
            with pe.Fori(0, NU) as u:
                pe.wait_ge(xm_ready, u + 1)
                pe.wait_ge(xt_ready, u * DB + 4)
                for c in range(DB):
                    for t in range(QT):
                        last = nc.tensor.transpose(bankT[c][:, t * P:(t + 1) * P], xm[:, t, c * P:(c + 1) * P], ident[:])
                    last.then_inc(xt_psum, 1)
                pe.wait_ge(xt_ready, u * DB + 8)
                for g in range(NG):
                    i = g % 4
                    pe.wait_ge(proj_used, u * NG + g + 1)
                    for c in range(DB):
                        if g < 2 * DB:
                            w = wk if g < DB else wq
                            last = nc.tensor.matmul(bankG[i][:], w[:, c, i * P:(i + 1) * P], xT[:, c, :], start=(c == 0), stop=(c == DB - 1))
                        else:
                            last = nc.tensor.matmul(bankG[i][:], xT[:, c, i * P:(i + 1) * P], wv[:, c, :], start=(c == 0), stop=(c == DB - 1))
                    last.then_inc(proj_ready, 1)


def phase_b(nc, sem, side, q_parts, k_parts, v_heads, pen_scratch, ctx_scratch, ident, sel4):
    R = 8
    HALF = S // 2
    TRIPS = NU * H // 2
    NT = TRIPS * R
    assert R == 2 * QT
    with ExitStack() as ctx:
        def sb(name, shape, dt=F32):
            return ctx.enter_context(nc.sbuf_tensor(name, shape, dt))

        ring = sb("ring", [P, R, S])
        keys = sb("keys", [P, 2, S], F32R)
        queries = sb("queries", [P, 2, TOK], F32R)
        values = sb("values", [P, 2, KB, DH])
        penb = sb("penb", [P, 2, QT, S], BF16)
        probT = sb("probT", [P, 2, KB, P])
        max_half = sb("max_half", [P, R, 2])
        neg_max = sb("neg_max", [P, R])
        sums = sb("sums", [P, R, 2])
        total = sb("total", [P, QT])
        recip = sb("recip", [P, QT])
        ctxp = sb("ctxp", [P, 2, P])
        ctx_out = sb("ctx_out", [P, 2, QT, DH])
        scores = [ctx.enter_context(nc.psum_tensor(f"scores{i}", [P, HALF], F32)) for i in range(2)]
        bankT = [ctx.enter_context(nc.psum_tensor(f"b_T{i}", [P, 4 * P], F32)) for i in range(2)]
        bank_ctx = ctx.enter_context(nc.psum_tensor("bank_ctx", [P, 4 * P], F32))
        bank_sum = ctx.enter_context(nc.psum_tensor("bank_sum", [P, 4 * P], F32))

        bias_in = [sem(f"bias_in{i}") for i in range(R)]
        pen_in = [[sem(f"pen_in{i}_{t}") for t in range(QT)] for i in range(2)]
        kq_in = [sem(f"kq_in{i}") for i in range(2)]
        v_in = [sem(f"v_in{i}") for i in range(2)]
        masked = sem("masked")
        scored = sem("scored")
        added = sem("added")
        max_ready = sem("max_ready")
        exp_done = sem("exp_done")
        turned = sem("turned")
        out_act = sem("out_act")
        out_dve = sem("out_dve")
        pv_done = sem("pv_done")
        ctx_copied = sem("ctx_copied")
        ctx_summed = sem("ctx_summed")
        ctx_normed = sem("ctx_normed")
        ctx_stored = [sem(f"ctx_stored{i}") for i in range(2)]
        norm_chain = sem("norm_chain")
        MASKED0, SCORED0, TURNED0, PV0 = 2 * H * QT, 4 * QT, 4 * R, 2 * QT

        block = ctx.enter_context(nc.Block())

        @block.sync
        def _(sp):
            with sp.Fori(0, B) as b:
                with sp.Fori(0, NS // 2) as s_pair:
                  for par in range(2):
                    s = s_pair * 2 + par
                    u = b * NS + s
                    for qt in range(QT):
                        sp.wait_ge(masked, u * H * QT + (MASKED0 - 2 * H * QT) + (H - 1) * QT + qt + 1)
                        sp.dma_start(penb[:, par, qt, :], pen_scratch[bass.ds(u, 1), :, qt * S:(qt + 1) * S].rearrange("o p n -> (o p) n")).then_inc(pen_in[par][qt], 16)
                    with sp.Fori(0, H // 2) as hp:
                        it = u * (H // 2) + hp
                        for j in range(R):
                            hh, qt = j // QT, j % QT
                            h, i, hd = hp * 2 + hh, it * R + j, it * 2 + hh
                            if qt == 0:
                                sp.wait_ge(scored, hd * 2 * QT + 2 * QT)
                                for n, (q_part, k_part) in enumerate(((0, 0), (1, 1), (0, 1), (1, 0))):
                                    sp.dma_start(queries[DH * n:DH * (n + 1), hh, :].bitcast(F32),
                                                 q_parts[bass.ds(b * 2 + q_part, 1), bass.ds(h * DH, DH), bass.ds(s * TOK, TOK)].rearrange("o d n -> (o d) n")).then_inc(kq_in[hh], 16)
                                    sp.dma_start(keys[DH * n:DH * (n + 1), hh, :].bitcast(F32),
                                                 k_parts[bass.ds(b * 2 + k_part, 1), bass.ds(h * DH, DH), :].rearrange("o d n -> (o d) n")).then_inc(kq_in[hh], 16)
                                sp.wait_ge(pv_done, hd * QT + QT)
                                sp.dma_start(values[:, hh, :, :].rearrange("p k d -> p (k d)"),
                                             v_heads[bass.ds(b, 1), bass.ds(h, 1)].rearrange("o h p n -> (o h p) n")).then_inc(v_in[hh], 16)
                            sp.wait_ge(turned, i * 4 + 4)
                            sp.dma_start(ring[:, j, :], side[bass.ds(b * H + h, 1), bass.ds((s * QT + qt) * P, P), :].rearrange("o q k -> (o q) k")).then_inc(bias_in[j], 16)
            for i in range(2):
                sp.wait_ge(ctx_stored[i], 16 + NU * H // 2 * 16)

        @block.gpsimd
        def _(pool):
            pool.sem_inc(masked, MASKED0)
            with pool.Fori(0, NU // 2) as u_pair:
                for par in range(2):
                    with pool.Fori(0, H // 2) as hp:
                        for j in range(R):
                            it = (u_pair * 2 + par) * (H // 2) + hp
                            pool.wait_ge(bias_in[j], it * 16 + 16)
                            pool.wait_ge(pen_in[par][j % QT], u_pair * 16 + 16)
                            nc.gpsimd.tensor_tensor(ring[:, j, :], ring[:, j, :], penb[:, par, j % QT, :], ALU.add).then_inc(masked, 1)

        def known(v):
            return isinstance(v, int)

        def live(tile):
            return not known(tile) or 0 <= tile < NT

        def need(eng, s, v):
            if not known(v) or v > 0:
                eng.wait_ge(s, v)

        def trips(eng, step):
            for j in range(R):
                step(0, j)
            with eng.Fori(1, TRIPS) as it:
                for j in range(R):
                    step(it, j)
            for j in range(QT + 1):
                step(TRIPS, j)

        @block.vector
        def _(dve):
            def step(it, j):
                i = it * R + j
                for half in range(2):
                    if live(i):
                        dve.wait_ge(scored, SCORED0 + i * 2 + half + 1)
                        if half == 0:
                            dve.wait_ge(masked, MASKED0 + i + 1)
                        else:
                            dve.wait_ge(added, i * 2 + 1)
                        dve.nop(nofuse=True)
                        at = ring[:, j, half * HALF:(half + 1) * HALF]
                        start = MASKED if half == 0 else max_half[:, j, 0:1]
                        nc.vector.tensor_tensor_reduce(out=at, in0=scores[half][:], in1=at, scale=1.0, scalar=start,
                                                       op0=ALU.add, op1=ALU.max,
                                                       accum_out=max_half[:, j, half:half + 1]).then_inc(added, 1)
                    if live(i - 2):
                        g = 2 * half + 1
                        dve.wait_ge(turned, TURNED0 + (i - 2) * 4 + g + 1)
                        dve.wait_ge(pv_done, PV0 + i - 3)
                        nc.vector.tensor_copy(probT[:, j % 2, 4 * g:4 * g + 4, :].rearrange("p c q -> p (c q)"),
                                              bankT[1][:]).then_inc(out_dve, 1)
                if live(i):
                    dve.wait_ge(added, i * 2 + 2)
                    nc.vector.tensor_scalar(neg_max[:, j:j + 1], max_half[:, j, 1:2], 4.0, -0.25,
                                            ALU.mult, ALU.mult).then_inc(max_ready, 1)
                if j % QT == QT - 1 and live(i - 7):
                    hd = it * 2 if j == 7 else it * 2 - 1
                    a = (j - 7) % R
                    hh = a // QT
                    link = chain(dve, norm_chain, hd * 2)
                    link(nc.vector.tensor_reduce(total[:], sums[:, a:a + QT, :], AXIS_X, ALU.add))
                    link(nc.vector.reciprocal(recip[:], total[:]))
                    dve.wait_ge(ctx_summed, i - 3)
                    stores = it if j == 7 else it - 1
                    dve.wait_ge(ctx_stored[hh], 16 + stores * 16)
                    nc.vector.tensor_tensor(ctx_out[:, hh, :, :], bank_sum[:, 0:P].rearrange("p (t d) -> p t d", t=QT),
                                            recip[:].rearrange("p (t o) -> p t o", o=1).to_broadcast([P, QT, DH]),
                                            ALU.mult).then_inc(ctx_normed, 1)

            trips(dve, step)

        @block.scalar
        def _(act):
            act.sem_inc(ctx_stored[0], 16)
            act.sem_inc(ctx_stored[1], 16)

            def step(it, j):
                i = it * R + j
                k = (j - 1) % R
                for half in range(2):
                    if live(i - 1):
                        if half == 0:
                            act.wait_ge(max_ready, i)
                        at = ring[:, k, half * HALF:(half + 1) * HALF]
                        nc.scalar.activation(at, at, ACT.Exp, bias=neg_max[:, k:k + 1],
                                             accum_out=sums[:, k, half:half + 1]).then_inc(exp_done, 1)
                    if live(i - 2):
                        g = 2 * half
                        act.wait_ge(turned, TURNED0 + (i - 2) * 4 + g + 1)
                        act.wait_ge(pv_done, PV0 + i - 3)
                        nc.scalar.copy(probT[:, j % 2, 4 * g:4 * g + 4, :].rearrange("p c q -> p (c q)"),
                                       bankT[0][:]).then_inc(out_act, 1)
                    if half == 0 and live(i - 3):
                        act.wait_ge(pv_done, PV0 + i - 2)
                        need(act, ctx_summed, i - 4)
                        nc.scalar.copy(ctxp[:, (j - 3) % 2, :], bank_ctx[:, 0:P]).then_inc(ctx_copied, 1)
                if j % QT == 0 and live(i - 8):
                    hd = it * 2 - 2 if j == 0 else it * 2 - 1
                    hh = j // QT
                    act.wait_ge(ctx_normed, hd + 1)
                    act.dma_start(ctx_scratch[bass.ds(hd, 1)].rearrange("o p n -> (o p) n"),
                                  ctx_out[:, hh, :, :].rearrange("p t d -> p (t d)")).then_inc(ctx_stored[hh], 16)

            trips(act, step)

        @block.tensor
        def _(pe):
            pe.sem_inc(scored, SCORED0)
            pe.sem_inc(turned, TURNED0)
            pe.sem_inc(pv_done, PV0)

            def score(it, j, half):
                i, hh = it * R + j, j // QT
                if live(i):
                    if j % QT == 0 and half == 0:
                        pe.wait_ge(kq_in[hh], it * 128 + 128)
                    need(pe, added, i * 2 - 1 + half)
                    for c in range(2):
                        at = half * HALF + c * 512
                        last = nc.tensor.matmul(scores[half][:, c * 512:(c + 1) * 512],
                                                queries[:, hh, (j % QT) * P:(j % QT + 1) * P],
                                                keys[:, hh, at:at + 512], start=True, stop=True)
                    last.then_inc(scored, 1)

            def turn(t, slot, g):
                if live(t):
                    if g % 2 == 0:
                        pe.wait_ge(exp_done, t * 2 + g // 2 + 1)
                    need(pe, out_dve if g % 2 else out_act, t * 2 + g // 2)
                    for c in range(4):
                        at = (4 * g + c) * P
                        last = nc.tensor.transpose(bankT[g % 2][:, c * P:(c + 1) * P], ring[:, slot, at:at + P], ident[:])
                    last.then_inc(turned, 1)

            def weigh(t, slot, trip, g):
                if live(t):
                    hh = slot // QT
                    if g == 0:
                        pe.wait_ge(v_in[hh], trip * 16 + 16)
                        need(pe, ctx_copied, t)
                    pe.wait_ge(out_dve if g % 2 else out_act, t * 2 + g // 2 + 1)
                    for c in range(4):
                        last = nc.tensor.matmul(bank_ctx[DH * c:DH * (c + 1), 0:P], values[:, hh, 4 * g + c, :],
                                                probT[:, slot % 2, 4 * g + c, :], start=(g == 0), stop=(g == 3))
                    if g == 3:
                        last.then_inc(pv_done, 1)

            def step(it, j):
                i = it * R + j
                two, three = (i - 2, (j - 2) % R), (i - 3, (j - 3) % R)
                trip2, trip3 = (it if j >= 2 else it - 1), (it if j >= 3 else it - 1)
                score(it, j, 0)
                turn(*two, 0)
                weigh(*three, trip3, 2)
                turn(*two, 1)
                weigh(*three, trip3, 3)
                score(it, j, 1)
                turn(*two, 2)
                weigh(*two, trip2, 0)
                turn(*two, 3)
                weigh(*two, trip2, 1)
                if live(i - 3):
                    t = (j - 3) % QT
                    pe.wait_ge(ctx_copied, i - 2)
                    if t == 0:
                        need(pe, ctx_normed, it * 2 if j == 3 else it * 2 + 1)
                    nc.tensor.matmul(bank_sum[:, t * DH:(t + 1) * DH], ctxp[:, (j - 3) % 2, :], sel4[:],
                                     start=True, stop=True).then_inc(ctx_summed, 1)

            trips(pe, step)


def phase_c(nc, sem, ctx_scratch, xm_scratch, Wo, bo, W1, b1, W2, b2, g2, beta2, out, ident, trig):
    with ExitStack() as ctx:
        def sb(name, shape, dt=F32):
            return ctx.enter_context(nc.sbuf_tensor(name, shape, dt))

        wo = sb("wo", [P, DB, D])
        w1 = sb("w1", [P, DB, F])
        w2 = sb("w2", [P, FB, D])
        b1_col = sb("b1_col", [P, FB])
        b1_scaled = sb("b1_scaled", [P, FB])
        bo_all, b2_all, g2_all, beta2_all = (sb(n, [P, D]) for n in ("bo_all", "b2_all", "g2_all", "beta2_all"))
        eps_c = sb("eps_c", [P, 1])
        cosines = sb("cosines", [P, B, 2])
        sines = sb("sines", [P, B, 2])
        ctx_in = sb("ctx_in", [P, QT, H, DH])
        xm_in = sb("xm_in", [P, QT, D])
        ctxT = sb("ctxT", [P, DB, TOK])
        x2 = sb("x2", [P, QT, D])
        stats = sb("stats_c", [P, QT, 6])
        mean_var = sb("mean_var_c", [P, QT, 2])
        std = sb("std_c", [P, QT])
        rstd = sb("rstd_c", [P, QT])
        hn = sb("hn", [P, QT, D])
        hT = sb("hT", [P, DB, TOK])
        gate = sb("gate", [P, 2, TOK])
        hidden = sb("hidden", [P, 4, TOK])
        y = sb("y", [P, 2, D])
        rot_a = sb("rot_a", [P, 2, D])
        rot_b = sb("rot_b", [P, 2, D])
        y_out = sb("y_out", [P, 2, D])
        acc = [ctx.enter_context(nc.psum_tensor(f"c_acc{i}", [P, D], F32)) for i in range(QT)]
        work = [ctx.enter_context(nc.psum_tensor(f"c_work{i}", [P, TOK], F32)) for i in range(4)]

        vec_in = sem("vec_in")
        wo_in, w1_in, w2_in = sem("wo_in"), sem("w1_in"), sem("w2_in")
        consts_ready = sem("consts_ready")
        ctx_ld, xm_ld = sem("ctx_ld"), sem("xm_ld")
        ctx_turned = sem("ctx_turned")
        ctxT_ready = sem("ctxT_ready")
        wo_done = sem("wo_done")
        x2_ready = sem("x2_ready")
        c_chain = sem("c_chain")
        c_var, c_std = sem("c_var"), sem("c_std")
        hn_ready = sem("hn_ready")
        h_turned = sem("h_turned")
        hT_ready = sem("hT_ready")
        up_done = sem("up_done")
        gate_ready = sem("gate_ready")
        hid_ready = sem("hid_ready")
        down_done = sem("down_done")
        acc_read = sem("acc_read")
        rotated = sem("rotated")
        y_ready = sem("y_ready")
        y_stored = [sem(f"y_stored{i}") for i in range(2)]

        block = ctx.enter_context(nc.Block())

        @block.sync
        def _(sp):
            def row(v):
                return v.rearrange("(o n) -> o n", o=1).to_broadcast([P, D])

            sp.dma_start(wo[:], Wo.rearrange("(c p) n -> p c n", p=P)).then_inc(wo_in, 16)
            for to, v in ((bo_all, bo), (b2_all, b2), (g2_all, g2), (beta2_all, beta2)):
                sp.dma_start(to[:], row(v)).then_inc(vec_in, 16)
            sp.dma_start(b1_col[:], b1.rearrange("(c p) -> p c", p=P), allow_slow_non_contiguous=True).then_inc(vec_in, 16)
            sp.sem_inc(y_stored[0], 16)
            sp.sem_inc(y_stored[1], 16)
            with sp.Fori(0, NU) as u:
                sp.wait_ge(ctx_turned, u * DB + 4)
                for t in range(QT):
                    sp.dma_start(ctx_in[:, t, :, :],
                                 ctx_scratch[bass.ds(u * H, H), :, t * DH:(t + 1) * DH].rearrange("h p d -> p h d")).then_inc(ctx_ld, 16)
                sp.wait_ge(x2_ready, u * QT + 4)
                sp.dma_start(xm_in[:].rearrange("p t n -> p (t n)"),
                             xm_scratch[bass.ds(u, 1)].rearrange("o p n -> (o p) n")).then_inc(xm_ld, 16)
                for t in range(QT):
                    sp.wait_ge(y_ready, u * QT + t + 3)
                    sp.dma_start(out[bass.ds(u, 1), t * P:(t + 1) * P, :].rearrange("o p n -> (o p) n"),
                                 y_out[:, t % 2, :]).then_inc(y_stored[t % 2], 16)
            for i in range(2):
                sp.wait_ge(y_stored[i], 16 + NU * QT // 2 * 16)

        @block.gpsimd
        def _(pool):
            for c in range(4):
                pool.dma_start(w1[:, :, c * D:(c + 1) * D], W1.rearrange("(c p) n -> p c n", p=P)[:, :, c * D:(c + 1) * D]).then_inc(w1_in, 16)
            for c in range(4):
                pool.dma_start(w2[:, 4 * c:4 * c + 4, :], W2.rearrange("(c p) n -> p c n", p=P)[:, 4 * c:4 * c + 4, :]).then_inc(w2_in, 16)
            pool.sem_inc(y_ready, 2)
            with pool.Fori(0, NU) as u:
                for t in range(QT):
                    pool.wait_ge(rotated, u * QT + t + 1)
                    pool.wait_ge(y_stored[t % 2], u * 32 + (t // 2) * 16 + 16)
                    nc.gpsimd.tensor_tensor(y_out[:, t % 2, :], rot_a[:, t % 2, :], rot_b[:, t % 2, :], ALU.add).then_inc(y_ready, 1)

        @block.scalar
        def _(act):
            act.wait_ge(consts_ready, 1)
            with act.Fori(0, NU) as u:
                for c in range(DB):
                    act.wait_ge(ctx_turned, u * DB + c + 5)
                    nc.scalar.copy(ctxT[:, c, :], work[c][:]).then_inc(ctxT_ready, 1)
                act.wait_ge(c_var, u + 1)
                nc.scalar.activation(std[:], mean_var[:, :, 1], ACT.Sqrt, bias=eps_c[:]).then_inc(c_std, 1)
                for c in range(DB):
                    act.wait_ge(h_turned, u * DB + c + 1)
                    nc.scalar.copy(hT[:, c, :], work[c][:]).then_inc(hT_ready, 1)
                for f in range(FB):
                    act.wait_ge(up_done, u * FB + f + 1)
                    act.wait_ge(hid_ready, u * FB + f + 3)
                    nc.scalar.activation(gate[:, f % 2, :], work[f % 4][:], ACT.Sigmoid, scale=1.702,
                                         bias=b1_scaled[:, f:f + 1]).then_inc(gate_ready, 1)

        @block.vector
        def _(dve):
            nc.vector.memset(eps_c[:], EPS)
            for b in range(B):
                for k in range(2):
                    nc.vector.tensor_copy(sines[:, b, k:k + 1], trig[:, 8 + 2 * k + b:9 + 2 * k + b])
                    nc.vector.tensor_copy(cosines[:, b, k:k + 1], trig[:, 12 + 2 * k + b:13 + 2 * k + b])
            dve.wait_ge(vec_in, 80)
            nc.vector.tensor_scalar(b1_scaled[:], b1_col[:], 1.702, None, ALU.mult).then_inc(consts_ready, 1)
            dve.wait_ge(consts_ready, 1)
            dve.sem_inc(x2_ready, 4)
            dve.sem_inc(hid_ready, 4)
            dve.sem_inc(acc_read, 4)
            LINKS = 6
            with dve.Fori(0, B) as b:
                with dve.Fori(0, NS) as s:
                    u = b * NS + s
                    link = chain(dve, c_chain, u * LINKS)
                    dve.wait_ge(xm_ld, u * 16 + 16)
                    for t in range(QT):
                        last = nc.vector.tensor_tensor(xm_in[:, t, :], xm_in[:, t, :], bo_all[:], ALU.add)
                    link(last)
                    for t in range(QT):
                        dve.wait_ge(wo_done, u * QT + t + 1)
                        nc.vector.tensor_tensor(x2[:, t, :], work[t][:], xm_in[:, t, :], ALU.add).then_inc(x2_ready, 1)
                    dve.wait_ge(x2_ready, u * QT + 8)
                    for t in range(QT):
                        last = nc.vector.bn_stats(stats[:, t, :], x2[:, t, :])
                    link(last)
                    dve.nop(nofuse=True)
                    for t in range(QT):
                        last = nc.vector.bn_aggr(mean_var[:, t, :], stats[:, t, :])
                    last.then_inc(c_var, 1)
                    dve.wait_ge(c_std, u + 1)
                    link(nc.vector.reciprocal(rstd[:], std[:]))
                    for t in range(QT):
                        last = nc.vector.tensor_scalar(hn[:, t, :], x2[:, t, :], mean_var[:, t, 0:1], rstd[:, t:t + 1], ALU.subtract, ALU.mult)
                    link(last)
                    for t in range(QT):
                        last = nc.vector.tensor_tensor(hn[:, t, :], hn[:, t, :], g2_all[:], ALU.mult)
                    link(last)
                    for t in range(QT):
                        last = nc.vector.tensor_tensor(hn[:, t, :], hn[:, t, :], beta2_all[:], ALU.add)
                    last.then_inc(hn_ready, 1)
                    for t in range(QT):
                        last = nc.vector.tensor_tensor(x2[:, t, :], x2[:, t, :], b2_all[:], ALU.add)
                    link(last)
                    for f in range(FB):
                        dve.wait_ge(gate_ready, u * FB + f + 1)
                        dve.wait_ge(down_done, u * FB + f + 1)
                        nc.vector.scalar_tensor_tensor(out=hidden[:, f % 4, :], in0=work[f % 4][:], scalar=b1_col[:, f:f + 1],
                                                       in1=gate[:, f % 2, :], op0=ALU.add, op1=ALU.mult).then_inc(hid_ready, 1)
                    dve.wait_ge(down_done, u * FB + FB + 4)
                    for t in range(QT):
                        r = t % 2
                        nc.vector.tensor_tensor(y[:, r, :], acc[t][:], x2[:, t, :], ALU.add).then_inc(acc_read, 1)
                        dve.wait_ge(acc_read, u * QT + t + 5)
                        dve.wait_ge(y_ready, u * QT + t + 1)
                        pairs = y[:, r, :].rearrange("p (n k e) -> p n k e", k=2, e=2)
                        to_a = rot_a[:, r, :].rearrange("p (n k e) -> p n k e", k=2, e=2)
                        to_b = rot_b[:, r, :].rearrange("p (n k e) -> p n k e", k=2, e=2)
                        for k in range(2):
                            cos_k = cosines[:, bass.ds(b, 1), k:k + 1].rearrange("p o n -> p (o n)")
                            sin_k = sines[:, bass.ds(b, 1), k:k + 1].rearrange("p o n -> p (o n)")
                            nc.vector.tensor_scalar(to_a[:, :, k, :], pairs[:, :, k, :], cos_k, None, ALU.mult)
                            nc.vector.tensor_scalar(to_b[:, :, k, 0], pairs[:, :, k, 1], sin_k, None, ALU.mult)
                            last = nc.vector.tensor_scalar(to_b[:, :, k, 1], pairs[:, :, k, 0], sin_k, -1.0, ALU.mult, ALU.mult)
                        last.then_inc(rotated, 1)
                    assert link.count[0] == LINKS

        @block.tensor
        def _(pe):
            pe.sem_inc(ctx_turned, 4)
            pe.sem_inc(down_done, 4)
            pe.wait_ge(wo_in, 16)
            with pe.Fori(0, NU) as u:
                pe.wait_ge(ctx_ld, u * 64 + 64)
                pe.wait_ge(hid_ready, u * FB + 4)
                for c in range(DB):
                    for t in range(QT):
                        last = nc.tensor.transpose(work[c][:, t * P:(t + 1) * P], ctx_in[:, t, 4 * c:4 * c + 4, :].rearrange("p h d -> p (h d)"), ident[:])
                    last.then_inc(ctx_turned, 1)
                pe.wait_ge(ctxT_ready, u * DB + 4)
                for t in range(QT):
                    for c in range(DB):
                        last = nc.tensor.matmul(work[t][:], ctxT[:, c, t * P:(t + 1) * P], wo[:, c, :], start=(c == 0), stop=(c == DB - 1))
                    last.then_inc(wo_done, 1)
                pe.wait_ge(hn_ready, u + 1)
                for c in range(DB):
                    for t in range(QT):
                        last = nc.tensor.transpose(work[c][:, t * P:(t + 1) * P], hn[:, t, c * P:(c + 1) * P], ident[:])
                    last.then_inc(h_turned, 1)
                pe.wait_ge(hT_ready, u * DB + 4)
                pe.wait_ge(w1_in, 64)
                pe.wait_ge(acc_read, u * QT + 4)
                for f in range(FB + 2):
                    if f < FB:
                        if f >= 4:
                            pe.wait_ge(hid_ready, u * FB + f + 1)
                        for c in range(DB):
                            last = nc.tensor.matmul(work[f % 4][:], w1[:, c, f * P:(f + 1) * P], hT[:, c, :], start=(c == 0), stop=(c == DB - 1))
                        last.then_inc(up_done, 1)
                    if f >= 2:
                        k = f - 2
                        pe.wait_ge(hid_ready, u * FB + k + 5)
                        if k == 0:
                            pe.wait_ge(w2_in, 64)
                        for t in range(QT):
                            last = nc.tensor.matmul(acc[t][:], hidden[:, k % 4, t * P:(t + 1) * P], w2[:, k, :], start=(k == 0), stop=(k == FB - 1))
                        last.then_inc(down_done, 1)


def build(nc, a, out):
    q_parts = nc.dram_tensor("q_parts", (B * 2, D, S), F32, kind="Internal").ap()
    k_parts = nc.dram_tensor("k_parts", (B * 2, D, S), F32, kind="Internal").ap()
    v_heads = nc.dram_tensor("v_heads", (B, H, P, KB * DH), F32, kind="Internal").ap()
    xm_scratch = nc.dram_tensor("xm_scratch", (NU, P, QT * D), F32, kind="Internal").ap()
    pen_scratch = nc.dram_tensor("pen_scratch", (NU, P, QT * S), BF16, kind="Internal").ap()
    ctx_scratch = nc.dram_tensor("ctx_scratch", (NU * H, P, QT * DH), F32, kind="Internal").ap()
    with ExitStack() as ctx:
        def sem(name):
            return ctx.enter_context(nc.semaphore(name))

        ident = ctx.enter_context(nc.sbuf_tensor("ident", [P, P], F32))
        sel4 = ctx.enter_context(nc.sbuf_tensor("sel4", [P, DH], F32))
        trig = ctx.enter_context(nc.sbuf_tensor("trig", [P, 16], F32))
        phase_a(nc, sem, a["x"], a["itok_B_34_63"], a["mask_Bx1xSxS_bk0"], a["condB_theta"], a["condB_phi"],
                a["L0_cond_W_ada"], a["L0_cond_b_ada"], a["L0_cond_Wq"], a["L0_cond_bq"], a["L0_cond_Wk"], a["L0_cond_bk"],
                a["L0_cond_Wv"], a["L0_cond_bv"], a["freqs"], q_parts, k_parts, v_heads, xm_scratch, pen_scratch,
                ident, sel4, trig)
        phase_b(nc, sem, a["fside_Bx16xSxS_0"], q_parts, k_parts, v_heads, pen_scratch, ctx_scratch, ident, sel4)
        phase_c(nc, sem, ctx_scratch, xm_scratch, a["L0_cond_Wo"], a["L0_cond_bo"], a["L0_cond_W1"], a["L0_cond_b1"],
                a["L0_cond_W2"], a["L0_cond_b2"], a["L0_cond_g2"], a["L0_cond_beta2"], out, ident, trig)


_VECTORS = ["itok_B_34_63", "condB_theta", "condB_phi"] + ["L0_cond_" + n for n in
            ("W_ada", "b_ada", "Wq", "bq", "Wk", "bk", "Wv", "bv", "Wo", "bo", "W1", "b1", "W2", "b2", "g2", "beta2")]


def kernel(**inputs):
    import numpy as _np
    import concourse.bacc as _bacc
    from concourse import mybir as _mybir
    from concourse.bass_utils import run_bass_kernel_spmd as _run

    nc = _bacc.Bacc("TRN2", target_bir_lowering=False, num_devices=1)
    arrays = {n: _np.ascontiguousarray(inputs[n]) for n in _VECTORS}
    arrays["x"] = _np.ascontiguousarray(inputs["x"]).reshape(NU, TOK, D)
    arrays["fside_Bx16xSxS_0"] = _np.ascontiguousarray(inputs["fside_Bx16xSxS_0"]).reshape(B * H, S, S)
    arrays["mask_Bx1xSxS_bk0"] = _np.ascontiguousarray(inputs["mask_Bx1xSxS_bk0"]).reshape(NU, TOK, S)
    half = D // 2
    arrays["freqs"] = _np.exp(_np.arange(half, dtype=_np.float32) * _np.float32(-math.log(10000.0) / (half - 1)))
    aps = {n: nc.dram_tensor(f"in_{n}", v.shape, _mybir.dt.from_np(v.dtype), kind="ExternalInput").ap() for n, v in arrays.items()}
    out = nc.dram_tensor("out_0", (NU, TOK, D), _mybir.dt.float32, kind="ExternalOutput").ap()
    build(nc, aps, out)
    r = _run(nc, [{f"in_{n}": v for n, v in arrays.items()}], core_ids=[0])
    return r.results[0]["out_0"].reshape(B, S, D)
```

```python
import math
from contextlib import ExitStack

import numpy as np

import concourse.bass as bass
from concourse import mybir

F32 = mybir.dt.float32
F32R = mybir.dt.float32r
BF16 = mybir.dt.bfloat16
U8 = mybir.dt.uint8
I32 = mybir.dt.int32
ALU = mybir.AluOpType
ACT = mybir.ActivationFunctionType
AXIS_X = mybir.AxisListType.X

P = 128
B, S, D, F = 2, 2048, 512, 2048
H = 16
DH = D // H
DB = D // P
FB = F // P
TOK = 512
QT = TOK // P
NS = S // TOK
NU = B * NS
KB = S // P
EPS = 1e-5
MASKED = -3.0e38
QSCALE = 1.0 / math.sqrt(DH)
NUM_STEPS, RESCALE = 100.0, 4000.0

TWO_PI_1 = 6.28125
TWO_PI_2 = float(np.float32(math.floor((2 * math.pi - TWO_PI_1) * 2**21) / 2**21))
TWO_PI_3 = 2 * math.pi - TWO_PI_1 - TWO_PI_2
ROUNDER = 1.5 * 2.0**23
SIN_MAX = 3.1415925


def chain(eng, sem, base):
    count = [0]

    def link(ins):
        count[0] += 1
        ins.then_inc(sem, 1)
        eng.wait_ge(sem, base + count[0])

    link.count = count
    return link


def phase_a(nc, sem, x, timestep, mask, theta, phi, W_ada, b_ada, Wq, bq, Wk, bk, Wv, bv, freqs,
            q_parts, k_parts, v_heads, xm_scratch, pen_scratch, ident, sel4, trig):
    with ExitStack() as ctx:
        def sb(name, shape, dt=F32):
            return ctx.enter_context(nc.sbuf_tensor(name, shape, dt))

        freq = sb("freq", [P, 2])
        t_int = sb("t_int", [P, B], I32)
        t_f32 = sb("t_f32", [P, B])
        angle = sb("angle", [P, 16])
        quarter = sb("quarter", [P, 16])
        turns = sb("turns", [P, 16])
        emb_sig = sb("emb_sig", [P, 8])
        emb_act = sb("emb_act", [P, 8])
        emb_wide = sb("emb_wide", [P, 8, P])
        w_ada = sb("w_ada", [P, DB, 2 * D])
        b_ada_all = sb("b_ada_all", [P, 2 * D])
        scale1 = sb("scale1", [P, B, D])
        shift = sb("shift", [P, B, D])
        wk = sb("wk", [P, DB, D])
        wq = sb("wq", [P, DB, D])
        wv = sb("wv", [P, DB, D])
        bq_col = sb("bq_col", [P, DB])
        bk_col = sb("bk_col", [P, DB])
        bv_all = sb("bv_all", [P, D])
        eps_a = sb("eps_a", [P, 1])
        xin = sb("xin", [P, QT, D])
        stats = sb("stats", [P, QT, 6])
        mean_var = sb("mean_var", [P, QT, 2])
        std = sb("std", [P, QT])
        rstd = sb("rstd", [P, QT])
        xm = sb("xm", [P, QT, D])
        xT = sb("xT", [P, DB, TOK])
        mask_in = sb("mask_in", [P, QT, S], U8)
        pen = sb("pen", [P, QT, S], BF16)
        exact = sb("exact", [P, 2, TOK])
        part_hi = sb("part_hi", [P, 4, TOK], F32R)
        part_lo = sb("part_lo", [P, 4, TOK], F32R)
        v_out = sb("v_out", [P, 4, D])
        bankT = [ctx.enter_context(nc.psum_tensor(f"a_T{i}", [P, TOK], F32)) for i in range(4)]
        bankG = [ctx.enter_context(nc.psum_tensor(f"a_G{i}", [P, TOK], F32)) for i in range(4)]

        const_ready = sem("const_ready")
        small_in = sem("small_in")
        w_ada_in = sem("w_ada_in")
        w_in = sem("w_in")
        a_chain = sem("a_chain")
        angles_ready = sem("angles_ready")
        sines_ready = sem("sines_ready")
        emb_ready = sem("emb_ready")
        ada_ready = sem("ada_ready")
        ada_used = sem("ada_used")
        x_in = sem("x_in")
        x_used = sem("x_used")
        var_ready = sem("var_ready")
        std_ready = sem("std_ready")
        ln_chain = sem("ln_chain")
        xm_ready = sem("xm_ready")
        xm_stored = sem("xm_stored")
        xt_psum = sem("xt_psum")
        xt_ready = sem("xt_ready")
        proj_ready = sem("proj_ready")
        proj_used = sem("proj_used")
        part_chain = sem("part_chain")
        staged = sem("staged")
        stored = [sem(f"stored{i}") for i in range(4)]
        mask_ld = sem("mask_ld")
        pen_ready = sem("pen_ready")
        pen_stored = sem("pen_stored")

        NG = 3 * DB
        STORES = 2 * 32 + 16

        block = ctx.enter_context(nc.Block())

        @block.gpsimd
        def _(pool):
            nc.gpsimd.memset(ident[:], 0.0).then_inc(const_ready, 1)
            nc.gpsimd.memset(sel4[:], 0.0).then_inc(const_ready, 1)
            pool.wait_ge(const_ready, 2)
            nc.gpsimd.affine_select(out=ident[:], in_=ident[:], compare_op=ALU.not_equal, fill=1.0,
                                    base=0, pattern=[[-1, P]], channel_multiplier=1).then_inc(const_ready, 1)
            for j in range(4):
                pool.wait_ge(const_ready, 3 + j)
                nc.gpsimd.affine_select(out=sel4[:], in_=sel4[:], compare_op=ALU.not_equal, fill=1.0,
                                        base=-DH * j, pattern=[[-1, DH]], channel_multiplier=1).then_inc(const_ready, 1)

        @block.sync
        def _(sp):
            sp.dma_start(freq[:], freqs.rearrange("(c p) -> p c", p=P), allow_slow_non_contiguous=True).then_inc(small_in, 16)
            sp.dma_start(t_int[:], timestep.rearrange("(o b) -> o b", o=1).to_broadcast([P, B])).then_inc(small_in, 16)
            for b in range(B):
                for c in (8 + b, 12 + b):
                    sp.dma_start(angle[:, c:c + 1], theta[b:b + 1].rearrange("(o b) -> o b", o=1).to_broadcast([P, 1]), allow_slow_non_contiguous=True).then_inc(small_in, 16)
                for c in (10 + b, 14 + b):
                    sp.dma_start(angle[:, c:c + 1], phi[b:b + 1].rearrange("(o b) -> o b", o=1).to_broadcast([P, 1]), allow_slow_non_contiguous=True).then_inc(small_in, 16)
            sp.dma_start(b_ada_all[:], b_ada.rearrange("(o n) -> o n", o=1).to_broadcast([P, 2 * D])).then_inc(small_in, 16)
            sp.dma_start(bq_col[:], bq.rearrange("(c p) -> p c", p=P), allow_slow_non_contiguous=True).then_inc(small_in, 16)
            sp.dma_start(bk_col[:], bk.rearrange("(c p) -> p c", p=P), allow_slow_non_contiguous=True).then_inc(small_in, 16)
            sp.dma_start(bv_all[:], bv.rearrange("(o n) -> o n", o=1).to_broadcast([P, D])).then_inc(small_in, 16)
            sp.dma_start(w_ada[:], W_ada.rearrange("(c p) n -> p c n", p=P)).then_inc(w_ada_in, 16)
            sp.dma_start(wk[:], Wk.rearrange("(c p) n -> p c n", p=P)).then_inc(w_in, 16)
            sp.dma_start(wq[:], Wq.rearrange("(c p) n -> p c n", p=P)).then_inc(w_in, 16)
            sp.dma_start(wv[:], Wv.rearrange("(c p) n -> p c n", p=P)).then_inc(w_in, 16)
            sp.sem_inc(xm_stored, 16)
            sp.sem_inc(pen_stored, 16)
            for i in range(4):
                sp.sem_inc(stored[i], 16)
            with sp.Fori(0, B) as b:
                with sp.Fori(0, NS) as s:
                    u = b * NS + s
                    sp.wait_ge(xm_ready, u + 1)
                    sp.dma_start(xm_scratch[bass.ds(u, 1)].rearrange("u p n -> (u p) n"),
                                 xm[:].rearrange("p t n -> p (t n)")).then_inc(xm_stored, 16)
                    for g in range(NG):
                        if g == 6:
                            sp.wait_ge(pen_ready, u * QT + QT)
                            sp.dma_start(pen_scratch[bass.ds(u, 1)].rearrange("u p n -> (u p) n"),
                                         pen[:].rearrange("p t n -> p (t n)")).then_inc(pen_stored, 16)
                        if g < 2 * DB:
                            sp.wait_ge(staged, u * 2 * DB + g + 1)
                        else:
                            sp.wait_ge(proj_used, u * NG + g + 5)
                        i = g % 4
                        if g < 2 * DB:
                            to = k_parts if g < DB else q_parts
                            for n, part in enumerate((part_hi, part_lo)):
                                sp.dma_start(to[bass.ds(b * 2 + n, 1), i * P:(i + 1) * P, bass.ds(s * TOK, TOK)].rearrange("o r n -> (o r) n"),
                                             part[:, i, :].bitcast(F32)).then_inc(stored[i], 16)
                        else:
                            sp.dma_start(v_heads[bass.ds(b * H, H), :, bass.ds((s * QT + i) * DH, DH)].rearrange("h p d -> p h d"),
                                         v_out[:, i, :].rearrange("p (h d) -> p h d", h=H)).then_inc(stored[i], 16)
            for i in range(4):
                sp.wait_ge(stored[i], 16 + NU * STORES)
            sp.wait_ge(xm_stored, 16 + NU * 16)
            sp.wait_ge(pen_stored, 16 + NU * 16)

        @block.scalar
        def _(act):
            act.wait_ge(angles_ready, 1)
            nc.scalar.activation(trig[:], angle[:], ACT.Sin).then_inc(sines_ready, 1)
            act.wait_ge(sines_ready, 1)
            nc.scalar.activation(emb_sig[:], trig[:, 0:8], ACT.Sigmoid).then_inc(sines_ready, 1)
            act.sem_inc(xt_ready, 4)
            with act.Fori(0, NU) as u:
                act.wait_ge(x_used, u + 1)
                act.dma_start(xin[:].rearrange("p t n -> p t n"),
                              x[bass.ds(u, 1)].rearrange("u (t p) n -> p (u t) n", p=P)).then_inc(x_in, 16)
                act.dma_start(mask_in[:], mask[bass.ds(u, 1)].rearrange("u (t p) n -> p (u t) n", p=P)).then_inc(mask_ld, 16)
                act.wait_ge(var_ready, u + 1)
                nc.scalar.activation(std[:], mean_var[:, :, 1], ACT.Sqrt, bias=eps_a[:]).then_inc(std_ready, 1)
                act.wait_ge(mask_ld, u * 16 + 16)
                act.wait_ge(pen_stored, u * 16 + 16)
                for t in range(QT):
                    nc.scalar.activation(pen[:, t, :], mask_in[:, t, :], ACT.Copy, scale=MASKED).then_inc(pen_ready, 1)
                act.wait_ge(pen_ready, u * QT + QT)
                for c in range(DB):
                    act.wait_ge(xt_psum, u * DB + c + 1 + 4)
                    act.wait_ge(proj_ready, u * NG + 12)
                    nc.scalar.copy(xT[:, c, :], bankT[c][:]).then_inc(xt_ready, 1)

        @block.vector
        def _(dve):
            link = chain(dve, a_chain, 0)
            nc.vector.memset(eps_a[:], EPS)
            nc.vector.memset(quarter[:, 0:4], 0.0)
            nc.vector.memset(quarter[:, 4:8], 0.25)
            nc.vector.memset(quarter[:, 8:12], 0.0)
            link(nc.vector.memset(quarter[:, 12:16], 0.25))
            dve.wait_ge(small_in, 14 * 16)
            link(nc.vector.tensor_copy(t_f32[:], t_int[:]))
            link(nc.vector.tensor_scalar(t_f32[:], t_f32[:], RESCALE / NUM_STEPS, None, ALU.mult))
            for k in range(2):
                for c in range(2):
                    last = nc.vector.tensor_scalar(angle[:, 4 * k + 2 * c:4 * k + 2 * c + 2], t_f32[:], freq[:, c:c + 1], None, ALU.mult)
            link(last)
            link(nc.vector.scalar_tensor_tensor(out=turns[:], in0=angle[:], scalar=1.0 / (2 * math.pi),
                                                in1=quarter[:], op0=ALU.mult, op1=ALU.add))
            link(nc.vector.tensor_scalar(turns[:], turns[:], ROUNDER, ROUNDER, ALU.add, ALU.subtract))
            for part in (TWO_PI_1, TWO_PI_2, TWO_PI_3):
                link(nc.vector.scalar_tensor_tensor(out=angle[:], in0=turns[:], scalar=-part,
                                                    in1=angle[:], op0=ALU.mult, op1=ALU.add))
            link(nc.vector.scalar_tensor_tensor(out=angle[:], in0=quarter[:], scalar=2 * math.pi,
                                                in1=angle[:], op0=ALU.mult, op1=ALU.add))
            nc.vector.tensor_scalar(angle[:], angle[:], SIN_MAX, -SIN_MAX, ALU.min, ALU.max).then_inc(angles_ready, 1)
            dve.wait_ge(sines_ready, 2)
            link(nc.vector.tensor_tensor(emb_act[:], trig[:, 0:8], emb_sig[:], ALU.mult))
            nc.vector.tensor_copy(emb_wide[:], emb_act[:].rearrange("p (c o) -> p c o", o=1).to_broadcast([P, 8, P])).then_inc(emb_ready, 1)
            for b in range(B):
                dve.wait_ge(ada_ready, 2 * b + 1)
                nc.vector.scalar_tensor_tensor(out=scale1[:, b, :], in0=bankG[2 * b][:], scalar=1.0,
                                               in1=b_ada_all[:, 0:D], op0=ALU.add, op1=ALU.add).then_inc(ada_used, 1)
                dve.wait_ge(ada_ready, 2 * b + 2)
                nc.vector.tensor_tensor(shift[:, b, :], bankG[2 * b + 1][:], b_ada_all[:, D:2 * D], ALU.add).then_inc(ada_used, 1)
            dve.sem_inc(x_used, 1)
            dve.sem_inc(proj_used, 4)
            dve.wait_ge(ada_used, 4)
            LN_LINKS, PART_LINKS = 3, 2 * DB
            with dve.Fori(0, B) as b:
                with dve.Fori(0, NS) as s:
                    u = b * NS + s
                    link = chain(dve, ln_chain, u * LN_LINKS)
                    dve.wait_ge(x_in, u * 16 + 16)
                    for t in range(QT):
                        last = nc.vector.bn_stats(stats[:, t, :], xin[:, t, :])
                    link(last)
                    dve.nop(nofuse=True)
                    for t in range(QT):
                        last = nc.vector.bn_aggr(mean_var[:, t, :], stats[:, t, :])
                    last.then_inc(var_ready, 1)
                    dve.wait_ge(std_ready, u + 1)
                    link(nc.vector.reciprocal(rstd[:], std[:]))
                    dve.wait_ge(xt_psum, u * DB + 4)
                    dve.wait_ge(xm_stored, u * 16 + 16)
                    for t in range(QT):
                        last = nc.vector.tensor_scalar(xm[:, t, :], xin[:, t, :], mean_var[:, t, 0:1], rstd[:, t:t + 1], ALU.subtract, ALU.mult)
                    last.then_inc(x_used, 1)
                    dve.wait_ge(x_used, u + 2)
                    for t in range(QT):
                        last = nc.vector.tensor_tensor(xm[:, t, :], xm[:, t, :], scale1[:, bass.ds(b, 1), :].rearrange("p o n -> p (o n)"), ALU.mult)
                    link(last)
                    for t in range(QT):
                        last = nc.vector.tensor_tensor(xm[:, t, :], xm[:, t, :], shift[:, bass.ds(b, 1), :].rearrange("p o n -> p (o n)"), ALU.add)
                    last.then_inc(xm_ready, 1)
                    assert link.count[0] == LN_LINKS
                    link = chain(dve, part_chain, u * PART_LINKS)
                    for g in range(NG):
                        i = g % 4
                        dve.wait_ge(proj_ready, u * NG + g + 1 + 12)
                        dve.wait_ge(stored[i], u * STORES + 32 * (g // 4) + 16)
                        if g < 2 * DB:
                            bias, scale = (bk_col, 1.0) if g < DB else (bq_col, QSCALE)
                            nc.vector.tensor_scalar(exact[:, g % 2, :], bankG[i][:], bias[:, i:i + 1], scale, ALU.add, ALU.mult).then_inc(proj_used, 1)
                            dve.wait_ge(proj_used, u * NG + g + 5)
                            link(nc.vector.tensor_copy(part_hi[:, i, :], exact[:, g % 2, :]))
                            nc.vector.tensor_tensor(part_lo[:, i, :], exact[:, g % 2, :], part_hi[:, i, :].bitcast(F32), ALU.subtract).then_inc(staged, 1)
                        else:
                            nc.vector.tensor_tensor(v_out[:, i, :], bankG[i][:], bv_all[:], ALU.add).then_inc(proj_used, 1)

        @block.tensor
        def _(pe):
            pe.wait_ge(emb_ready, 1)
            pe.wait_ge(w_ada_in, 16)
            for b in range(B):
                for half in range(2):
                    for c in range(DB):
                        last = nc.tensor.matmul(bankG[2 * b + half][:], emb_wide[:, 2 * c + b, :],
                                                w_ada[:, c, half * D:(half + 1) * D], start=(c == 0), stop=(c == DB - 1))
                    last.then_inc(ada_ready, 1)
            pe.sem_inc(xt_psum, 4)
            pe.sem_inc(proj_ready, 12)
            pe.wait_ge(const_ready, 7)
            pe.wait_ge(ada_used, 4)
            pe.wait_ge(w_in, 48)
            with pe.Fori(0, NU) as u:
                pe.wait_ge(xm_ready, u + 1)
                pe.wait_ge(xt_ready, u * DB + 4)
                for c in range(DB):
                    for t in range(QT):
                        last = nc.tensor.transpose(bankT[c][:, t * P:(t + 1) * P], xm[:, t, c * P:(c + 1) * P], ident[:])
                    last.then_inc(xt_psum, 1)
                pe.wait_ge(xt_ready, u * DB + 8)
                for g in range(NG):
                    i = g % 4
                    pe.wait_ge(proj_used, u * NG + g + 1)
                    for c in range(DB):
                        if g < 2 * DB:
                            w = wk if g < DB else wq
                            last = nc.tensor.matmul(bankG[i][:], w[:, c, i * P:(i + 1) * P], xT[:, c, :], start=(c == 0), stop=(c == DB - 1))
                        else:
                            last = nc.tensor.matmul(bankG[i][:], xT[:, c, i * P:(i + 1) * P], wv[:, c, :], start=(c == 0), stop=(c == DB - 1))
                    last.then_inc(proj_ready, 1)


def phase_b(nc, sem, side, q_parts, k_parts, v_heads, pen_scratch, ctx_scratch, ident, sel4):
    R = 8
    CH = 2
    CW = S // CH
    N = 512
    QR = KB // 4
    GROUPS = B * S // (R * P)
    TRIPS = GROUPS * H
    NT = TRIPS * R
    UNITS = TRIPS * 2
    assert R == 2 * QT and QR * P == N
    with ExitStack() as ctx:
        def sb(name, shape, dt=F32):
            return ctx.enter_context(nc.sbuf_tensor(name, shape, dt))

        ring = sb("ring", [P, R, S])
        keys = sb("keys", [P, 2, S], F32R)
        queries = sb("queries", [P, 2, TOK], F32R)
        values = sb("values", [P, 2, KB, DH])
        penb = sb("penb", [P, R, S], BF16)
        probT = sb("probT", [P, 2, KB, TOK])
        max_part = sb("max_part", [P, R, CH])
        neg_max = sb("neg_max", [P, R])
        sums = sb("sums", [P, R])
        all_masked = sb("all_masked", [P, QT])
        total = sb("total", [P, QT])
        recip = sb("recip", [P, 2, QT])
        ctxp = sb("ctxp", [P, TOK])
        ctx_out = sb("ctx_out", [P, 2, QT, DH])
        scores = [ctx.enter_context(nc.psum_tensor(f"scores{i}", [P, CW], F32)) for i in range(CH)]
        bankT = [ctx.enter_context(nc.psum_tensor(f"b_T{i}", [P, N], F32)) for i in range(2)]
        bank_ctx = ctx.enter_context(nc.psum_tensor("bank_ctx", [P, TOK], F32))
        bank_sum = ctx.enter_context(nc.psum_tensor("bank_sum", [P, TOK], F32))

        bias_in = [sem(f"bias_in{i}") for i in range(R)]
        pen_in = [sem(f"pen_in{i}") for i in range(R)]
        k_in = sem("k_in")
        q_in = [sem(f"q_in{i}") for i in range(2)]
        v_in = [sem(f"v_in{i}") for i in range(2)]
        masked = sem("masked")
        scored = sem("scored")
        added = sem("added")
        max_ready = sem("max_ready")
        exp_done = sem("exp_done")
        turned = sem("turned")
        out_act = sem("out_act")
        out_dve = sem("out_dve")
        pv_done = sem("pv_done")
        ctx_copied = sem("ctx_copied")
        ctx_summed = sem("ctx_summed")
        recip_ready = sem("recip_ready")
        ctx_normed = sem("ctx_normed")
        ctx_stored = [sem(f"ctx_stored{i}") for i in range(2)]
        SCORED0, TURNED0, PV0 = 2 * R * CH, 4 * R, 2

        block = ctx.enter_context(nc.Block())

        @block.sync
        def _(sp):
            def load_head(b, pair, h, first):
                it = (b * (GROUPS // B) + pair) * H + h
                for j in range(R):
                    i, hh, qt = it * R + j, j // QT, j % QT
                    sp.wait_ge(turned, i * 4 + 4)
                    sp.dma_start(ring[:, j, :], side[bass.ds(b * H + h, 1), bass.ds((pair * R + j) * P, P), :].rearrange("o q k -> (o q) k")).then_inc(bias_in[j], 16)
                    if first:
                        sp.dma_start(penb[:, j, :], pen_scratch[bass.ds(b * NS + pair * 2 + hh, 1), :, qt * S:(qt + 1) * S].rearrange("o p n -> (o p) n")).then_inc(pen_in[j], 16)
                    if j == 0:
                        sp.wait_ge(scored, it * R * CH + R * CH)
                        for n, part in enumerate((0, 1, 1, 0)):
                            sp.dma_start(keys[DH * n:DH * (n + 1), bass.ds(it % 2, 1), :].rearrange("p o n -> p (o n)").bitcast(F32),
                                         k_parts[bass.ds(b * 2 + part, 1), bass.ds(h * DH, DH), :].rearrange("o d n -> (o d) n")).then_inc(k_in, 16)
                    if qt == 2:
                        sp.wait_ge(scored, it * R * CH + (R + QT * (1 + hh)) * CH)
                        for n, part in enumerate((0, 1, 0, 1)):
                            sp.dma_start(queries[DH * n:DH * (n + 1), hh, :].bitcast(F32),
                                         q_parts[bass.ds(b * 2 + part, 1), bass.ds(h * DH, DH), bass.ds((pair * 2 + hh) * TOK, TOK)].rearrange("o d n -> (o d) n")).then_inc(q_in[hh], 16)

            with sp.Fori(0, B) as b:
                with sp.Fori(0, GROUPS // B) as pair:
                    load_head(b, pair, 0, True)
                    with sp.Fori(1, H) as h:
                        load_head(b, pair, h, False)
            for i in range(2):
                sp.wait_ge(ctx_stored[i], 16 + TRIPS * 16)

        @block.gpsimd
        def _(pool):
            with pool.Fori(0, GROUPS) as g:
                with pool.Fori(0, H) as h:
                    for j in range(R):
                        pool.wait_ge(bias_in[j], (g * H + h) * 16 + 16)
                        pool.wait_ge(pen_in[j], g * 16 + 16)
                        nc.gpsimd.tensor_tensor(ring[:, j, :], ring[:, j, :], penb[:, j, :], ALU.add).then_inc(masked, 1)

        def known(v):
            return isinstance(v, int)

        def live(number, count):
            return not known(number) or 0 <= number < count

        def need(eng, s, v):
            if not known(v) or v > 0:
                eng.wait_ge(s, v)

        def trips(eng, step):
            for j in range(R):
                step(0, j)
            with eng.Fori(1, TRIPS) as it:
                for j in range(R):
                    step(it, j)
            for j in range(R):
                step(TRIPS, j)

        def closing(it, j):
            return it * 2 - 2 if j < QT else it * 2 - 1

        @block.vector
        def _(dve):
            dve.sem_inc(ctx_normed, 1)

            def copy_quarter(it, j, n):
                t, k = it * R + j - 2, (j - 2) % R
                hh, q = k // QT, k % QT
                if live(t, NT):
                    dve.wait_ge(turned, TURNED0 + t * 4 + n + 1)
                    if q == 0 and n == 2:
                        dve.wait_ge(pv_done, PV0 - 1 + (it * 2 if j == 2 else it * 2 + 1))
                    nc.vector.tensor_copy(probT[:, hh, QR * n:QR * (n + 1), q * P:(q + 1) * P],
                                          bankT[n - 2][:].rearrange("p (c q) -> p c q", c=QR)).then_inc(out_dve, 1)

            def add(it, j, c):
                i = it * R + j
                if live(i, NT):
                    dve.wait_ge(scored, SCORED0 + i * CH + c + 1)
                    if c == 0:
                        dve.wait_ge(masked, i + 1)
                    else:
                        dve.wait_ge(added, i * CH + c)
                    dve.nop(nofuse=True)
                    at = ring[:, j, c * CW:(c + 1) * CW]
                    nc.vector.tensor_tensor_reduce(out=at, in0=scores[c][:], in1=at, scale=1.0,
                                                   scalar=max_part[:, j, c - 1:c] if c else MASKED,
                                                   op0=ALU.add, op1=ALU.max,
                                                   accum_out=max_part[:, j, c:c + 1]).then_inc(added, 1)

            def step(it, j):
                i = it * R + j
                unit, hh = closing(it, j) + 1, 1 if j < QT else 0
                dividing = j % QT == 1 and live(unit, UNITS)
                add(it, j, 0)
                if dividing:
                    nc.vector.tensor_scalar(all_masked[:], neg_max[:, hh * QT:(hh + 1) * QT], 4.0, 0.0, ALU.mult, ALU.mult).then_inc(recip_ready, 1)
                add(it, j, 1)
                if dividing:
                    dve.wait_ge(exp_done, i - 1)
                    dve.wait_ge(recip_ready, unit * 3 + 1)
                    nc.vector.tensor_tensor(total[:], sums[:, hh * QT:(hh + 1) * QT], all_masked[:], ALU.add).then_inc(recip_ready, 1)
                if live(i, NT):
                    dve.wait_ge(added, i * CH + CH)
                    nc.vector.tensor_scalar(neg_max[:, j:j + 1], max_part[:, j, CH - 1:CH], -1.0, None, ALU.mult).then_inc(max_ready, 1)
                copy_quarter(it, j, 2)
                if dividing:
                    dve.wait_ge(recip_ready, unit * 3 + 2)
                    nc.vector.reciprocal(recip[:, hh, :], total[:]).then_inc(recip_ready, 1)
                copy_quarter(it, j, 3)
                if j % QT == 2:
                    unit, hh = closing(it, j), 0 if j < QT else 1
                    if live(unit, UNITS):
                        dve.wait_ge(ctx_summed, unit + 2)
                        dve.wait_ge(recip_ready, unit * 3 + 3)
                        dve.wait_ge(ctx_stored[hh], it * 16)
                        nc.vector.tensor_tensor(ctx_out[:, hh, :, :], bank_sum[:, 0:P].rearrange("p (t d) -> p t d", t=QT),
                                                recip[:, hh, :].rearrange("p (t o) -> p t o", o=1).to_broadcast([P, QT, DH]),
                                                ALU.mult).then_inc(ctx_normed, 1)

            trips(dve, step)

        @block.scalar
        def _(act):
            def load_values(it, hh):
                batch, h = it // (TRIPS // B), it % H
                act.dma_start(values[:, hh, :, :].rearrange("p k d -> p (k d)"),
                              v_heads[bass.ds(batch * H + h, 1)].rearrange("o p n -> (o p) n")).then_inc(v_in[hh], 16)

            act.sem_inc(ctx_stored[0], 16)
            act.sem_inc(ctx_stored[1], 16)
            load_values(0, 0)
            load_values(0, 1)

            def step(it, j):
                i = it * R + j
                if live(i - 1, NT):
                    k = (j - 1) % R
                    act.wait_ge(max_ready, i)
                    nc.scalar.activation(ring[:, k, :], ring[:, k, :], ACT.Exp, bias=neg_max[:, k:k + 1],
                                         accum_out=sums[:, k:k + 1]).then_inc(exp_done, 1)
                if live(i - 2, NT):
                    hh, q = ((j - 2) % R) // QT, (j - 2) % QT
                    for n in (0, 1):
                        act.wait_ge(turned, TURNED0 + (i - 2) * 4 + n + 1)
                        if q == 0 and n == 0:
                            act.wait_ge(pv_done, PV0 - 1 + (it * 2 if j == 2 else it * 2 + 1))
                        nc.scalar.copy(probT[:, hh, QR * n:QR * (n + 1), q * P:(q + 1) * P],
                                       bankT[n][:].rearrange("p (c q) -> p c q", c=QR)).then_inc(out_act, 1)
                if j % QT == 1:
                    unit = closing(it, j)
                    if live(unit, UNITS):
                        act.wait_ge(pv_done, PV0 + unit + 1)
                        act.wait_ge(ctx_summed, unit + 1)
                        nc.scalar.copy(ctxp[:], bank_ctx[:]).then_inc(ctx_copied, 1)
                        if not known(it) or it < TRIPS:
                            load_values(it, 0 if j < QT else 1)
                if j % QT == 3:
                    unit, hh = closing(it, j), 0 if j < QT else 1
                    if live(unit, UNITS):
                        trip = it - 1
                        act.wait_ge(ctx_normed, unit + 2)
                        act.dma_start(ctx_scratch[bass.ds((trip // H) * 2 * H + hh * H + trip % H, 1)].rearrange("o p n -> (o p) n"),
                                      ctx_out[:, hh, :, :].rearrange("p t d -> p (t d)")).then_inc(ctx_stored[hh], 16)

            trips(act, step)

        @block.tensor
        def _(pe):
            pe.sem_inc(scored, SCORED0)
            pe.sem_inc(turned, TURNED0)
            pe.sem_inc(pv_done, PV0)
            pe.sem_inc(ctx_summed, 1)

            def score(it, j, c):
                i, hh, q = it * R + j, j // QT, j % QT
                if live(i, NT):
                    if j == 0 and c == 0:
                        pe.wait_ge(k_in, it * 64 + 64)
                    if q == 0 and c == 0:
                        pe.wait_ge(q_in[hh], it * 64 + 64)
                    need(pe, added, i * CH + c - 1)
                    for n in range(CW // N):
                        last = nc.tensor.matmul(scores[c][:, n * N:(n + 1) * N], queries[:, hh, q * P:(q + 1) * P],
                                                keys[:, bass.ds(it % 2, 1), c * CW + n * N:c * CW + (n + 1) * N].rearrange("p o n -> p (o n)"),
                                                start=True, stop=True)
                    last.then_inc(scored, 1)

            def turn(it, j, n):
                t, slot = it * R + j - 2, (j - 2) % R
                if live(t, NT):
                    if n == 0:
                        pe.wait_ge(exp_done, t + 1)
                    if n < 2:
                        need(pe, out_dve, t * 2 - 1 + n)
                    else:
                        pe.wait_ge(out_act, t * 2 - 1 + n)
                    for c in range(QR):
                        at = (QR * n + c) * P
                        last = nc.tensor.transpose(bankT[n % 2][:, c * P:(c + 1) * P], ring[:, slot, at:at + P], ident[:])
                    last.then_inc(turned, 1)

            def weigh(it, j):
                n = (j - 2) % QT
                unit = it * 2 - 2 if j < 2 else it * 2 - 1 if j < 6 else it * 2
                hh = 1 if 2 <= j < 6 else 0
                if live(unit, UNITS):
                    if n == 0:
                        pe.wait_ge(v_in[hh], it * 16 if j == 2 else it * 16 + 16)
                        need(pe, ctx_copied, unit)
                    pe.wait_ge(out_act if n < 2 else out_dve, (unit * QT + QT - 1) * 2 + n % 2 + 1)
                    for c in range(4):
                        last = nc.tensor.matmul(bank_ctx[DH * c:DH * (c + 1), :], values[:, hh, QR * n + c, :],
                                                probT[:, hh, QR * n + c, :], start=(n == 0), stop=(n == 3))
                    if n == 3:
                        last.then_inc(pv_done, 1)

            def close(it, j):
                unit = closing(it, j)
                if live(unit, UNITS):
                    pe.wait_ge(ctx_copied, unit + 1)
                    pe.wait_ge(ctx_normed, unit + 1)
                    for t in range(QT):
                        last = nc.tensor.matmul(bank_sum[:, t * DH:(t + 1) * DH], ctxp[:, t * P:(t + 1) * P], sel4[:],
                                                start=True, stop=True)
                    last.then_inc(ctx_summed, 1)

            def step(it, j):
                score(it, j, 0)
                score(it, j, 1)
                turn(it, j, 0)
                turn(it, j, 1)
                if j % QT == 2:
                    close(it, j)
                weigh(it, j)
                turn(it, j, 2)
                turn(it, j, 3)

            trips(pe, step)


def phase_c(nc, sem, ctx_scratch, xm_scratch, Wo, bo, W1, b1, W2, b2, g2, beta2, out, ident, trig):
    with ExitStack() as ctx:
        def sb(name, shape, dt=F32):
            return ctx.enter_context(nc.sbuf_tensor(name, shape, dt))

        wo = sb("wo", [P, DB, D])
        w1 = sb("w1", [P, DB, F])
        w2 = sb("w2", [P, FB, D])
        b1_col = sb("b1_col", [P, FB])
        b1_scaled = sb("b1_scaled", [P, FB])
        bo_all, b2_all, g2_all, beta2_all = (sb(n, [P, D]) for n in ("bo_all", "b2_all", "g2_all", "beta2_all"))
        eps_c = sb("eps_c", [P, 1])
        cosines = sb("cosines", [P, B, 2])
        sines = sb("sines", [P, B, 2])
        ctx_in = sb("ctx_in", [P, QT, H, DH])
        xm_in = sb("xm_in", [P, QT, D])
        ctxT = sb("ctxT", [P, DB, TOK])
        x2 = sb("x2", [P, QT, D])
        stats = sb("stats_c", [P, QT, 6])
        mean_var = sb("mean_var_c", [P, QT, 2])
        std = sb("std_c", [P, QT])
        rstd = sb("rstd_c", [P, QT])
        hn = sb("hn", [P, QT, D])
        hT = sb("hT", [P, DB, TOK])
        gate = sb("gate", [P, 2, TOK])
        hidden = sb("hidden", [P, 4, TOK])
        y = sb("y", [P, 2, D])
        rot_a = sb("rot_a", [P, 2, D])
        rot_b = sb("rot_b", [P, 2, D])
        y_out = sb("y_out", [P, 2, D])
        acc = [ctx.enter_context(nc.psum_tensor(f"c_acc{i}", [P, D], F32)) for i in range(QT)]
        work = [ctx.enter_context(nc.psum_tensor(f"c_work{i}", [P, TOK], F32)) for i in range(4)]

        vec_in = sem("vec_in")
        wo_in, w1_in, w2_in = sem("wo_in"), sem("w1_in"), sem("w2_in")
        consts_ready = sem("consts_ready")
        ctx_ld, xm_ld = sem("ctx_ld"), sem("xm_ld")
        ctx_turned = sem("ctx_turned")
        ctxT_ready = sem("ctxT_ready")
        wo_done = sem("wo_done")
        x2_ready = sem("x2_ready")
        c_chain = sem("c_chain")
        c_var, c_std = sem("c_var"), sem("c_std")
        hn_ready = sem("hn_ready")
        h_turned = sem("h_turned")
        hT_ready = sem("hT_ready")
        up_done = sem("up_done")
        gate_ready = sem("gate_ready")
        hid_ready = sem("hid_ready")
        down_done = sem("down_done")
        acc_read = sem("acc_read")
        rotated = sem("rotated")
        y_ready = sem("y_ready")
        y_stored = [sem(f"y_stored{i}") for i in range(2)]

        block = ctx.enter_context(nc.Block())

        @block.sync
        def _(sp):
            def row(v):
                return v.rearrange("(o n) -> o n", o=1).to_broadcast([P, D])

            sp.dma_start(wo[:], Wo.rearrange("(c p) n -> p c n", p=P)).then_inc(wo_in, 16)
            for to, v in ((bo_all, bo), (b2_all, b2), (g2_all, g2), (beta2_all, beta2)):
                sp.dma_start(to[:], row(v)).then_inc(vec_in, 16)
            sp.dma_start(b1_col[:], b1.rearrange("(c p) -> p c", p=P), allow_slow_non_contiguous=True).then_inc(vec_in, 16)
            sp.sem_inc(y_stored[0], 16)
            sp.sem_inc(y_stored[1], 16)
            with sp.Fori(0, NU) as u:
                sp.wait_ge(ctx_turned, u * DB + 4)
                for t in range(QT):
                    sp.dma_start(ctx_in[:, t, :, :],
                                 ctx_scratch[bass.ds(u * H, H), :, t * DH:(t + 1) * DH].rearrange("h p d -> p h d")).then_inc(ctx_ld, 16)
                sp.wait_ge(x2_ready, u * QT + 4)
                sp.dma_start(xm_in[:].rearrange("p t n -> p (t n)"),
                             xm_scratch[bass.ds(u, 1)].rearrange("o p n -> (o p) n")).then_inc(xm_ld, 16)
                for t in range(QT):
                    sp.wait_ge(y_ready, u * QT + t + 3)
                    sp.dma_start(out[bass.ds(u, 1), t * P:(t + 1) * P, :].rearrange("o p n -> (o p) n"),
                                 y_out[:, t % 2, :]).then_inc(y_stored[t % 2], 16)
            for i in range(2):
                sp.wait_ge(y_stored[i], 16 + NU * QT // 2 * 16)

        @block.gpsimd
        def _(pool):
            for c in range(4):
                pool.dma_start(w1[:, :, c * D:(c + 1) * D], W1.rearrange("(c p) n -> p c n", p=P)[:, :, c * D:(c + 1) * D]).then_inc(w1_in, 16)
            for c in range(4):
                pool.dma_start(w2[:, 4 * c:4 * c + 4, :], W2.rearrange("(c p) n -> p c n", p=P)[:, 4 * c:4 * c + 4, :]).then_inc(w2_in, 16)
            pool.sem_inc(y_ready, 2)
            with pool.Fori(0, NU) as u:
                for t in range(QT):
                    pool.wait_ge(rotated, u * QT + t + 1)
                    pool.wait_ge(y_stored[t % 2], u * 32 + (t // 2) * 16 + 16)
                    nc.gpsimd.tensor_tensor(y_out[:, t % 2, :], rot_a[:, t % 2, :], rot_b[:, t % 2, :], ALU.add).then_inc(y_ready, 1)

        @block.scalar
        def _(act):
            act.wait_ge(consts_ready, 1)
            with act.Fori(0, NU) as u:
                for c in range(DB):
                    act.wait_ge(ctx_turned, u * DB + c + 5)
                    nc.scalar.copy(ctxT[:, c, :], work[c][:]).then_inc(ctxT_ready, 1)
                act.wait_ge(c_var, u + 1)
                nc.scalar.activation(std[:], mean_var[:, :, 1], ACT.Sqrt, bias=eps_c[:]).then_inc(c_std, 1)
                for c in range(DB):
                    act.wait_ge(h_turned, u * DB + c + 1)
                    nc.scalar.copy(hT[:, c, :], work[c][:]).then_inc(hT_ready, 1)
                for f in range(FB):
                    act.wait_ge(up_done, u * FB + f + 1)
                    act.wait_ge(hid_ready, u * FB + f + 3)
                    nc.scalar.activation(gate[:, f % 2, :], work[f % 4][:], ACT.Sigmoid, scale=1.702,
                                         bias=b1_scaled[:, f:f + 1]).then_inc(gate_ready, 1)

        @block.vector
        def _(dve):
            nc.vector.memset(eps_c[:], EPS)
            for b in range(B):
                for k in range(2):
                    nc.vector.tensor_copy(sines[:, b, k:k + 1], trig[:, 8 + 2 * k + b:9 + 2 * k + b])
                    nc.vector.tensor_copy(cosines[:, b, k:k + 1], trig[:, 12 + 2 * k + b:13 + 2 * k + b])
            dve.wait_ge(vec_in, 80)
            nc.vector.tensor_scalar(b1_scaled[:], b1_col[:], 1.702, None, ALU.mult).then_inc(consts_ready, 1)
            dve.wait_ge(consts_ready, 1)
            dve.sem_inc(x2_ready, 4)
            dve.sem_inc(hid_ready, 4)
            dve.sem_inc(acc_read, 4)
            LINKS = 6
            with dve.Fori(0, B) as b:
                with dve.Fori(0, NS) as s:
                    u = b * NS + s
                    link = chain(dve, c_chain, u * LINKS)
                    dve.wait_ge(xm_ld, u * 16 + 16)
                    for t in range(QT):
                        last = nc.vector.tensor_tensor(xm_in[:, t, :], xm_in[:, t, :], bo_all[:], ALU.add)
                    link(last)
                    for t in range(QT):
                        dve.wait_ge(wo_done, u * QT + t + 1)
                        nc.vector.tensor_tensor(x2[:, t, :], work[t][:], xm_in[:, t, :], ALU.add).then_inc(x2_ready, 1)
                    dve.wait_ge(x2_ready, u * QT + 8)
                    for t in range(QT):
                        last = nc.vector.bn_stats(stats[:, t, :], x2[:, t, :])
                    link(last)
                    dve.nop(nofuse=True)
                    for t in range(QT):
                        last = nc.vector.bn_aggr(mean_var[:, t, :], stats[:, t, :])
                    last.then_inc(c_var, 1)
                    dve.wait_ge(c_std, u + 1)
                    link(nc.vector.reciprocal(rstd[:], std[:]))
                    for t in range(QT):
                        last = nc.vector.tensor_scalar(hn[:, t, :], x2[:, t, :], mean_var[:, t, 0:1], rstd[:, t:t + 1], ALU.subtract, ALU.mult)
                    link(last)
                    for t in range(QT):
                        last = nc.vector.tensor_tensor(hn[:, t, :], hn[:, t, :], g2_all[:], ALU.mult)
                    link(last)
                    for t in range(QT):
                        last = nc.vector.tensor_tensor(hn[:, t, :], hn[:, t, :], beta2_all[:], ALU.add)
                    last.then_inc(hn_ready, 1)
                    for t in range(QT):
                        last = nc.vector.tensor_tensor(x2[:, t, :], x2[:, t, :], b2_all[:], ALU.add)
                    link(last)
                    for f in range(FB):
                        dve.wait_ge(gate_ready, u * FB + f + 1)
                        dve.wait_ge(down_done, u * FB + f + 1)
                        nc.vector.scalar_tensor_tensor(out=hidden[:, f % 4, :], in0=work[f % 4][:], scalar=b1_col[:, f:f + 1],
                                                       in1=gate[:, f % 2, :], op0=ALU.add, op1=ALU.mult).then_inc(hid_ready, 1)
                    dve.wait_ge(down_done, u * FB + FB + 4)
                    for t in range(QT):
                        r = t % 2
                        nc.vector.tensor_tensor(y[:, r, :], acc[t][:], x2[:, t, :], ALU.add).then_inc(acc_read, 1)
                        dve.wait_ge(acc_read, u * QT + t + 5)
                        dve.wait_ge(y_ready, u * QT + t + 1)
                        pairs = y[:, r, :].rearrange("p (n k e) -> p n k e", k=2, e=2)
                        to_a = rot_a[:, r, :].rearrange("p (n k e) -> p n k e", k=2, e=2)
                        to_b = rot_b[:, r, :].rearrange("p (n k e) -> p n k e", k=2, e=2)
                        for k in range(2):
                            cos_k = cosines[:, bass.ds(b, 1), k:k + 1].rearrange("p o n -> p (o n)")
                            sin_k = sines[:, bass.ds(b, 1), k:k + 1].rearrange("p o n -> p (o n)")
                            nc.vector.tensor_scalar(to_a[:, :, k, :], pairs[:, :, k, :], cos_k, None, ALU.mult)
                            nc.vector.tensor_scalar(to_b[:, :, k, 0], pairs[:, :, k, 1], sin_k, None, ALU.mult)
                            last = nc.vector.tensor_scalar(to_b[:, :, k, 1], pairs[:, :, k, 0], sin_k, -1.0, ALU.mult, ALU.mult)
                        last.then_inc(rotated, 1)
                    assert link.count[0] == LINKS

        @block.tensor
        def _(pe):
            pe.sem_inc(ctx_turned, 4)
            pe.sem_inc(down_done, 4)
            pe.wait_ge(wo_in, 16)
            with pe.Fori(0, NU) as u:
                pe.wait_ge(ctx_ld, u * 64 + 64)
                pe.wait_ge(hid_ready, u * FB + 4)
                for c in range(DB):
                    for t in range(QT):
                        last = nc.tensor.transpose(work[c][:, t * P:(t + 1) * P], ctx_in[:, t, 4 * c:4 * c + 4, :].rearrange("p h d -> p (h d)"), ident[:])
                    last.then_inc(ctx_turned, 1)
                pe.wait_ge(ctxT_ready, u * DB + 4)
                for t in range(QT):
                    for c in range(DB):
                        last = nc.tensor.matmul(work[t][:], ctxT[:, c, t * P:(t + 1) * P], wo[:, c, :], start=(c == 0), stop=(c == DB - 1))
                    last.then_inc(wo_done, 1)
                pe.wait_ge(hn_ready, u + 1)
                for c in range(DB):
                    for t in range(QT):
                        last = nc.tensor.transpose(work[c][:, t * P:(t + 1) * P], hn[:, t, c * P:(c + 1) * P], ident[:])
                    last.then_inc(h_turned, 1)
                pe.wait_ge(hT_ready, u * DB + 4)
                pe.wait_ge(w1_in, 64)
                pe.wait_ge(acc_read, u * QT + 4)
                for f in range(FB + 2):
                    if f < FB:
                        if f >= 4:
                            pe.wait_ge(hid_ready, u * FB + f + 1)
                        for c in range(DB):
                            last = nc.tensor.matmul(work[f % 4][:], w1[:, c, f * P:(f + 1) * P], hT[:, c, :], start=(c == 0), stop=(c == DB - 1))
                        last.then_inc(up_done, 1)
                    if f >= 2:
                        k = f - 2
                        pe.wait_ge(hid_ready, u * FB + k + 5)
                        if k == 0:
                            pe.wait_ge(w2_in, 64)
                        for t in range(QT):
                            last = nc.tensor.matmul(acc[t][:], hidden[:, k % 4, t * P:(t + 1) * P], w2[:, k, :], start=(k == 0), stop=(k == FB - 1))
                        last.then_inc(down_done, 1)


def build(nc, a, out):
    q_parts = nc.dram_tensor("q_parts", (B * 2, D, S), F32, kind="Internal").ap()
    k_parts = nc.dram_tensor("k_parts", (B * 2, D, S), F32, kind="Internal").ap()
    v_heads = nc.dram_tensor("v_heads", (B * H, P, KB * DH), F32, kind="Internal").ap()
    xm_scratch = nc.dram_tensor("xm_scratch", (NU, P, QT * D), F32, kind="Internal").ap()
    pen_scratch = nc.dram_tensor("pen_scratch", (NU, P, QT * S), BF16, kind="Internal").ap()
    ctx_scratch = nc.dram_tensor("ctx_scratch", (NU * H, P, QT * DH), F32, kind="Internal").ap()
    with ExitStack() as ctx:
        def sem(name):
            return ctx.enter_context(nc.semaphore(name))

        ident = ctx.enter_context(nc.sbuf_tensor("ident", [P, P], F32))
        sel4 = ctx.enter_context(nc.sbuf_tensor("sel4", [P, DH], F32))
        trig = ctx.enter_context(nc.sbuf_tensor("trig", [P, 16], F32))
        phase_a(nc, sem, a["x"], a["itok_B_34_63"], a["mask_Bx1xSxS_bk0"], a["condB_theta"], a["condB_phi"],
                a["L0_cond_W_ada"], a["L0_cond_b_ada"], a["L0_cond_Wq"], a["L0_cond_bq"], a["L0_cond_Wk"], a["L0_cond_bk"],
                a["L0_cond_Wv"], a["L0_cond_bv"], a["freqs"], q_parts, k_parts, v_heads, xm_scratch, pen_scratch,
                ident, sel4, trig)
        phase_b(nc, sem, a["fside_Bx16xSxS_0"], q_parts, k_parts, v_heads, pen_scratch, ctx_scratch, ident, sel4)
        phase_c(nc, sem, ctx_scratch, xm_scratch, a["L0_cond_Wo"], a["L0_cond_bo"], a["L0_cond_W1"], a["L0_cond_b1"],
                a["L0_cond_W2"], a["L0_cond_b2"], a["L0_cond_g2"], a["L0_cond_beta2"], out, ident, trig)


_VECTORS = ["itok_B_34_63", "condB_theta", "condB_phi"] + ["L0_cond_" + n for n in
            ("W_ada", "b_ada", "Wq", "bq", "Wk", "bk", "Wv", "bv", "Wo", "bo", "W1", "b1", "W2", "b2", "g2", "beta2")]


def kernel(**inputs):
    import numpy as _np
    import concourse.bacc as _bacc
    from concourse import mybir as _mybir
    from concourse.bass_utils import run_bass_kernel_spmd as _run

    nc = _bacc.Bacc("TRN2", target_bir_lowering=False, num_devices=1)
    arrays = {n: _np.ascontiguousarray(inputs[n]) for n in _VECTORS}
    arrays["x"] = _np.ascontiguousarray(inputs["x"]).reshape(NU, TOK, D)
    arrays["fside_Bx16xSxS_0"] = _np.ascontiguousarray(inputs["fside_Bx16xSxS_0"]).reshape(B * H, S, S)
    arrays["mask_Bx1xSxS_bk0"] = _np.ascontiguousarray(inputs["mask_Bx1xSxS_bk0"]).reshape(NU, TOK, S)
    half = D // 2
    arrays["freqs"] = _np.exp(_np.arange(half, dtype=_np.float32) * _np.float32(-math.log(10000.0) / (half - 1)))
    aps = {n: nc.dram_tensor(f"in_{n}", v.shape, _mybir.dt.from_np(v.dtype), kind="ExternalInput").ap() for n, v in arrays.items()}
    out = nc.dram_tensor("out_0", (NU, TOK, D), _mybir.dt.float32, kind="ExternalOutput").ap()
    build(nc, aps, out)
    r = _run(nc, [{f"in_{n}": v for n, v in arrays.items()}], core_ids=[0])
    return r.results[0]["out_0"].reshape(B, S, D)
```

```python
import math
from contextlib import ExitStack

import numpy as np

import concourse.bass as bass
from concourse import mybir

F32 = mybir.dt.float32
F32R = mybir.dt.float32r
BF16 = mybir.dt.bfloat16
U8 = mybir.dt.uint8
I32 = mybir.dt.int32
ALU = mybir.AluOpType
ACT = mybir.ActivationFunctionType
AXIS_X = mybir.AxisListType.X

P = 128
B, S, D, F = 2, 2048, 512, 2048
H = 16
DH = D // H
DB = D // P
FB = F // P
TOK = 512
QT = TOK // P
NS = S // TOK
NU = B * NS
KB = S // P
EPS = 1e-5
MASKED = -3.0e38
QSCALE = 1.0 / math.sqrt(DH)
NUM_STEPS, RESCALE = 100.0, 4000.0

TWO_PI_1 = 6.28125
TWO_PI_2 = float(np.float32(math.floor((2 * math.pi - TWO_PI_1) * 2**21) / 2**21))
TWO_PI_3 = 2 * math.pi - TWO_PI_1 - TWO_PI_2
ROUNDER = 1.5 * 2.0**23
SIN_MAX = 3.1415925


def chain(eng, sem, base):
    count = [0]

    def link(ins):
        count[0] += 1
        ins.then_inc(sem, 1)
        eng.wait_ge(sem, base + count[0])

    link.count = count
    return link


def phase_a(nc, sem, x, timestep, mask, theta, phi, W_ada, b_ada, Wq, bq, Wk, bk, Wv, bv, freqs,
            q_parts, k_parts, v_heads, xm_scratch, pen_scratch, ident, sel4, trig):
    with ExitStack() as ctx:
        def sb(name, shape, dt=F32):
            return ctx.enter_context(nc.sbuf_tensor(name, shape, dt))

        freq = sb("freq", [P, 2])
        t_int = sb("t_int", [P, B], I32)
        t_f32 = sb("t_f32", [P, B])
        angle = sb("angle", [P, 16])
        quarter = sb("quarter", [P, 16])
        turns = sb("turns", [P, 16])
        emb_sig = sb("emb_sig", [P, 8])
        emb_act = sb("emb_act", [P, 8])
        emb_wide = sb("emb_wide", [P, 8, P])
        w_ada = sb("w_ada", [P, DB, 2 * D])
        b_ada_all = sb("b_ada_all", [P, 2 * D])
        scale1 = sb("scale1", [P, B, D])
        shift = sb("shift", [P, B, D])
        wk = sb("wk", [P, DB, D])
        wq = sb("wq", [P, DB, D])
        wv = sb("wv", [P, DB, D])
        bq_col = sb("bq_col", [P, DB])
        bk_col = sb("bk_col", [P, DB])
        bv_all = sb("bv_all", [P, D])
        eps_a = sb("eps_a", [P, 1])
        xin = sb("xin", [P, QT, D])
        stats = sb("stats", [P, QT, 6])
        mean_var = sb("mean_var", [P, QT, 2])
        std = sb("std", [P, QT])
        rstd = sb("rstd", [P, QT])
        xm = sb("xm", [P, QT, D])
        xT = sb("xT", [P, DB, TOK])
        mask_in = sb("mask_in", [P, QT, S], U8)
        pen = sb("pen", [P, QT, S], BF16)
        exact = sb("exact", [P, 2, TOK])
        part_hi = sb("part_hi", [P, 4, TOK], F32R)
        part_lo = sb("part_lo", [P, 4, TOK], F32R)
        v_out = sb("v_out", [P, 4, D])
        bankT = [ctx.enter_context(nc.psum_tensor(f"a_T{i}", [P, TOK], F32)) for i in range(4)]
        bankG = [ctx.enter_context(nc.psum_tensor(f"a_G{i}", [P, TOK], F32)) for i in range(4)]

        const_ready = sem("const_ready")
        small_in = sem("small_in")
        w_ada_in = sem("w_ada_in")
        w_in = sem("w_in")
        a_chain = sem("a_chain")
        angles_ready = sem("angles_ready")
        sines_ready = sem("sines_ready")
        emb_ready = sem("emb_ready")
        ada_ready = sem("ada_ready")
        ada_used = sem("ada_used")
        x_in = sem("x_in")
        x_used = sem("x_used")
        var_ready = sem("var_ready")
        std_ready = sem("std_ready")
        ln_chain = sem("ln_chain")
        xm_ready = sem("xm_ready")
        xm_stored = sem("xm_stored")
        xt_psum = sem("xt_psum")
        xt_ready = sem("xt_ready")
        proj_ready = sem("proj_ready")
        proj_used = sem("proj_used")
        part_chain = sem("part_chain")
        staged = sem("staged")
        stored = [sem(f"stored{i}") for i in range(4)]
        mask_ld = sem("mask_ld")
        pen_ready = sem("pen_ready")
        pen_stored = sem("pen_stored")

        NG = 3 * DB
        STORES = 2 * 32 + 16

        block = ctx.enter_context(nc.Block())

        @block.gpsimd
        def _(pool):
            nc.gpsimd.memset(ident[:], 0.0).then_inc(const_ready, 1)
            nc.gpsimd.memset(sel4[:], 0.0).then_inc(const_ready, 1)
            pool.wait_ge(const_ready, 2)
            nc.gpsimd.affine_select(out=ident[:], in_=ident[:], compare_op=ALU.not_equal, fill=1.0,
                                    base=0, pattern=[[-1, P]], channel_multiplier=1).then_inc(const_ready, 1)
            for j in range(4):
                pool.wait_ge(const_ready, 3 + j)
                nc.gpsimd.affine_select(out=sel4[:], in_=sel4[:], compare_op=ALU.not_equal, fill=1.0,
                                        base=-DH * j, pattern=[[-1, DH]], channel_multiplier=1).then_inc(const_ready, 1)

        @block.sync
        def _(sp):
            sp.dma_start(freq[:], freqs.rearrange("(c p) -> p c", p=P), allow_slow_non_contiguous=True).then_inc(small_in, 16)
            sp.dma_start(t_int[:], timestep.rearrange("(o b) -> o b", o=1).to_broadcast([P, B])).then_inc(small_in, 16)
            for b in range(B):
                for c in (8 + b, 12 + b):
                    sp.dma_start(angle[:, c:c + 1], theta[b:b + 1].rearrange("(o b) -> o b", o=1).to_broadcast([P, 1]), allow_slow_non_contiguous=True).then_inc(small_in, 16)
                for c in (10 + b, 14 + b):
                    sp.dma_start(angle[:, c:c + 1], phi[b:b + 1].rearrange("(o b) -> o b", o=1).to_broadcast([P, 1]), allow_slow_non_contiguous=True).then_inc(small_in, 16)
            sp.dma_start(b_ada_all[:], b_ada.rearrange("(o n) -> o n", o=1).to_broadcast([P, 2 * D])).then_inc(small_in, 16)
            sp.dma_start(bq_col[:], bq.rearrange("(c p) -> p c", p=P), allow_slow_non_contiguous=True).then_inc(small_in, 16)
            sp.dma_start(bk_col[:], bk.rearrange("(c p) -> p c", p=P), allow_slow_non_contiguous=True).then_inc(small_in, 16)
            sp.dma_start(bv_all[:], bv.rearrange("(o n) -> o n", o=1).to_broadcast([P, D])).then_inc(small_in, 16)
            sp.dma_start(w_ada[:], W_ada.rearrange("(c p) n -> p c n", p=P)).then_inc(w_ada_in, 16)
            sp.dma_start(wk[:], Wk.rearrange("(c p) n -> p c n", p=P)).then_inc(w_in, 16)
            sp.dma_start(wq[:], Wq.rearrange("(c p) n -> p c n", p=P)).then_inc(w_in, 16)
            sp.dma_start(wv[:], Wv.rearrange("(c p) n -> p c n", p=P)).then_inc(w_in, 16)
            sp.sem_inc(xm_stored, 16)
            sp.sem_inc(pen_stored, 16)
            for i in range(4):
                sp.sem_inc(stored[i], 16)
            with sp.Fori(0, B) as b:
                with sp.Fori(0, NS) as s:
                    u = b * NS + s
                    sp.wait_ge(xm_ready, u + 1)
                    sp.dma_start(xm_scratch[bass.ds(u, 1)].rearrange("u p n -> (u p) n"),
                                 xm[:].rearrange("p t n -> p (t n)")).then_inc(xm_stored, 16)
                    for g in range(NG):
                        if g == 6:
                            sp.wait_ge(pen_ready, u * QT + QT)
                            sp.dma_start(pen_scratch[bass.ds(u, 1)].rearrange("u p n -> (u p) n"),
                                         pen[:].rearrange("p t n -> p (t n)")).then_inc(pen_stored, 16)
                        if g < 2 * DB:
                            sp.wait_ge(staged, u * 2 * DB + g + 1)
                        else:
                            sp.wait_ge(proj_used, u * NG + g + 5)
                        i = g % 4
                        if g < 2 * DB:
                            to = k_parts if g < DB else q_parts
                            for n, part in enumerate((part_hi, part_lo)):
                                sp.dma_start(to[bass.ds(b * 2 + n, 1), i * P:(i + 1) * P, bass.ds(s * TOK, TOK)].rearrange("o r n -> (o r) n"),
                                             part[:, i, :].bitcast(F32)).then_inc(stored[i], 16)
                        else:
                            sp.dma_start(v_heads[bass.ds(b * H, H), :, bass.ds((s * QT + i) * DH, DH)].rearrange("h p d -> p h d"),
                                         v_out[:, i, :].rearrange("p (h d) -> p h d", h=H)).then_inc(stored[i], 16)
            for i in range(4):
                sp.wait_ge(stored[i], 16 + NU * STORES)
            sp.wait_ge(xm_stored, 16 + NU * 16)
            sp.wait_ge(pen_stored, 16 + NU * 16)

        @block.scalar
        def _(act):
            act.wait_ge(angles_ready, 1)
            nc.scalar.activation(trig[:], angle[:], ACT.Sin).then_inc(sines_ready, 1)
            act.wait_ge(sines_ready, 1)
            nc.scalar.activation(emb_sig[:], trig[:, 0:8], ACT.Sigmoid).then_inc(sines_ready, 1)
            act.sem_inc(xt_ready, 4)
            with act.Fori(0, NU) as u:
                act.wait_ge(x_used, u + 1)
                act.dma_start(xin[:].rearrange("p t n -> p t n"),
                              x[bass.ds(u, 1)].rearrange("u (t p) n -> p (u t) n", p=P)).then_inc(x_in, 16)
                act.dma_start(mask_in[:], mask[bass.ds(u, 1)].rearrange("u (t p) n -> p (u t) n", p=P)).then_inc(mask_ld, 16)
                act.wait_ge(var_ready, u + 1)
                nc.scalar.activation(std[:], mean_var[:, :, 1], ACT.Sqrt, bias=eps_a[:]).then_inc(std_ready, 1)
                act.wait_ge(mask_ld, u * 16 + 16)
                act.wait_ge(pen_stored, u * 16 + 16)
                for t in range(QT):
                    nc.scalar.activation(pen[:, t, :], mask_in[:, t, :], ACT.Copy, scale=MASKED).then_inc(pen_ready, 1)
                act.wait_ge(pen_ready, u * QT + QT)
                for c in range(DB):
                    act.wait_ge(xt_psum, u * DB + c + 1 + 4)
                    act.wait_ge(proj_ready, u * NG + 12)
                    nc.scalar.copy(xT[:, c, :], bankT[c][:]).then_inc(xt_ready, 1)

        @block.vector
        def _(dve):
            link = chain(dve, a_chain, 0)
            nc.vector.memset(eps_a[:], EPS)
            nc.vector.memset(quarter[:, 0:4], 0.0)
            nc.vector.memset(quarter[:, 4:8], 0.25)
            nc.vector.memset(quarter[:, 8:12], 0.0)
            link(nc.vector.memset(quarter[:, 12:16], 0.25))
            dve.wait_ge(small_in, 14 * 16)
            link(nc.vector.tensor_copy(t_f32[:], t_int[:]))
            link(nc.vector.tensor_scalar(t_f32[:], t_f32[:], RESCALE / NUM_STEPS, None, ALU.mult))
            for k in range(2):
                for c in range(2):
                    last = nc.vector.tensor_scalar(angle[:, 4 * k + 2 * c:4 * k + 2 * c + 2], t_f32[:], freq[:, c:c + 1], None, ALU.mult)
            link(last)
            link(nc.vector.scalar_tensor_tensor(out=turns[:], in0=angle[:], scalar=1.0 / (2 * math.pi),
                                                in1=quarter[:], op0=ALU.mult, op1=ALU.add))
            link(nc.vector.tensor_scalar(turns[:], turns[:], ROUNDER, ROUNDER, ALU.add, ALU.subtract))
            for part in (TWO_PI_1, TWO_PI_2, TWO_PI_3):
                link(nc.vector.scalar_tensor_tensor(out=angle[:], in0=turns[:], scalar=-part,
                                                    in1=angle[:], op0=ALU.mult, op1=ALU.add))
            link(nc.vector.scalar_tensor_tensor(out=angle[:], in0=quarter[:], scalar=2 * math.pi,
                                                in1=angle[:], op0=ALU.mult, op1=ALU.add))
            nc.vector.tensor_scalar(angle[:], angle[:], SIN_MAX, -SIN_MAX, ALU.min, ALU.max).then_inc(angles_ready, 1)
            dve.wait_ge(sines_ready, 2)
            link(nc.vector.tensor_tensor(emb_act[:], trig[:, 0:8], emb_sig[:], ALU.mult))
            nc.vector.tensor_copy(emb_wide[:], emb_act[:].rearrange("p (c o) -> p c o", o=1).to_broadcast([P, 8, P])).then_inc(emb_ready, 1)
            for b in range(B):
                dve.wait_ge(ada_ready, 2 * b + 1)
                nc.vector.scalar_tensor_tensor(out=scale1[:, b, :], in0=bankG[2 * b][:], scalar=1.0,
                                               in1=b_ada_all[:, 0:D], op0=ALU.add, op1=ALU.add).then_inc(ada_used, 1)
                dve.wait_ge(ada_ready, 2 * b + 2)
                nc.vector.tensor_tensor(shift[:, b, :], bankG[2 * b + 1][:], b_ada_all[:, D:2 * D], ALU.add).then_inc(ada_used, 1)
            dve.sem_inc(x_used, 1)
            dve.sem_inc(proj_used, 4)
            dve.wait_ge(ada_used, 4)
            LN_LINKS, PART_LINKS = 3, 2 * DB
            with dve.Fori(0, B) as b:
                with dve.Fori(0, NS) as s:
                    u = b * NS + s
                    link = chain(dve, ln_chain, u * LN_LINKS)
                    dve.wait_ge(x_in, u * 16 + 16)
                    for t in range(QT):
                        last = nc.vector.bn_stats(stats[:, t, :], xin[:, t, :])
                    link(last)
                    dve.nop(nofuse=True)
                    for t in range(QT):
                        last = nc.vector.bn_aggr(mean_var[:, t, :], stats[:, t, :])
                    last.then_inc(var_ready, 1)
                    dve.wait_ge(std_ready, u + 1)
                    link(nc.vector.reciprocal(rstd[:], std[:]))
                    dve.wait_ge(xt_psum, u * DB + 4)
                    dve.wait_ge(xm_stored, u * 16 + 16)
                    for t in range(QT):
                        last = nc.vector.tensor_scalar(xm[:, t, :], xin[:, t, :], mean_var[:, t, 0:1], rstd[:, t:t + 1], ALU.subtract, ALU.mult)
                    last.then_inc(x_used, 1)
                    dve.wait_ge(x_used, u + 2)
                    for t in range(QT):
                        last = nc.vector.tensor_tensor(xm[:, t, :], xm[:, t, :], scale1[:, bass.ds(b, 1), :].rearrange("p o n -> p (o n)"), ALU.mult)
                    link(last)
                    for t in range(QT):
                        last = nc.vector.tensor_tensor(xm[:, t, :], xm[:, t, :], shift[:, bass.ds(b, 1), :].rearrange("p o n -> p (o n)"), ALU.add)
                    last.then_inc(xm_ready, 1)
                    assert link.count[0] == LN_LINKS
                    link = chain(dve, part_chain, u * PART_LINKS)
                    for g in range(NG):
                        i = g % 4
                        dve.wait_ge(proj_ready, u * NG + g + 1 + 12)
                        dve.wait_ge(stored[i], u * STORES + 32 * (g // 4) + 16)
                        if g < 2 * DB:
                            bias, scale = (bk_col, 1.0) if g < DB else (bq_col, QSCALE)
                            nc.vector.tensor_scalar(exact[:, g % 2, :], bankG[i][:], bias[:, i:i + 1], scale, ALU.add, ALU.mult).then_inc(proj_used, 1)
                            dve.wait_ge(proj_used, u * NG + g + 5)
                            link(nc.vector.tensor_copy(part_hi[:, i, :], exact[:, g % 2, :]))
                            nc.vector.tensor_tensor(part_lo[:, i, :], exact[:, g % 2, :], part_hi[:, i, :].bitcast(F32), ALU.subtract).then_inc(staged, 1)
                        else:
                            nc.vector.tensor_tensor(v_out[:, i, :], bankG[i][:], bv_all[:], ALU.add).then_inc(proj_used, 1)

        @block.tensor
        def _(pe):
            pe.wait_ge(emb_ready, 1)
            pe.wait_ge(w_ada_in, 16)
            for b in range(B):
                for half in range(2):
                    for c in range(DB):
                        last = nc.tensor.matmul(bankG[2 * b + half][:], emb_wide[:, 2 * c + b, :],
                                                w_ada[:, c, half * D:(half + 1) * D], start=(c == 0), stop=(c == DB - 1))
                    last.then_inc(ada_ready, 1)
            pe.sem_inc(xt_psum, 4)
            pe.sem_inc(proj_ready, 12)
            pe.wait_ge(const_ready, 7)
            pe.wait_ge(ada_used, 4)
            pe.wait_ge(w_in, 48)
            with pe.Fori(0, NU) as u:
                pe.wait_ge(xm_ready, u + 1)
                pe.wait_ge(xt_ready, u * DB + 4)
                for c in range(DB):
                    for t in range(QT):
                        last = nc.tensor.transpose(bankT[c][:, t * P:(t + 1) * P], xm[:, t, c * P:(c + 1) * P], ident[:])
                    last.then_inc(xt_psum, 1)
                pe.wait_ge(xt_ready, u * DB + 8)
                for g in range(NG):
                    i = g % 4
                    pe.wait_ge(proj_used, u * NG + g + 1)
                    for c in range(DB):
                        if g < 2 * DB:
                            w = wk if g < DB else wq
                            last = nc.tensor.matmul(bankG[i][:], w[:, c, i * P:(i + 1) * P], xT[:, c, :], start=(c == 0), stop=(c == DB - 1))
                        else:
                            last = nc.tensor.matmul(bankG[i][:], xT[:, c, i * P:(i + 1) * P], wv[:, c, :], start=(c == 0), stop=(c == DB - 1))
                    last.then_inc(proj_ready, 1)


def phase_b(nc, sem, side, q_parts, k_parts, v_heads, pen_scratch, ctx_scratch, ident, sel4):
    R = 8
    CH = 2
    CW = S // CH
    N = 512
    QR = KB // 4
    GROUPS = B * S // (R * P)
    TRIPS = GROUPS * H
    NT = TRIPS * R
    UNITS = TRIPS * 2
    assert R == 2 * QT and QR * P == N
    with ExitStack() as ctx:
        def sb(name, shape, dt=F32):
            return ctx.enter_context(nc.sbuf_tensor(name, shape, dt))

        ring = sb("ring", [P, R, S])
        keys = sb("keys", [P, 2, S], F32R)
        queries = sb("queries", [P, 2, TOK], F32R)
        values = sb("values", [P, 2, KB, DH])
        penb = sb("penb", [P, R, S], BF16)
        probT = sb("probT", [P, 2, KB, TOK])
        max_part = sb("max_part", [P, R, CH])
        neg_max = sb("neg_max", [P, R])
        sums = sb("sums", [P, R])
        all_masked = sb("all_masked", [P, QT])
        total = sb("total", [P, QT])
        recip = sb("recip", [P, 2, QT])
        ctxp = sb("ctxp", [P, TOK])
        ctx_out = sb("ctx_out", [P, 2, QT, DH])
        scores = [ctx.enter_context(nc.psum_tensor(f"scores{i}", [P, CW], F32)) for i in range(CH)]
        bankT = [ctx.enter_context(nc.psum_tensor(f"b_T{i}", [P, N], F32)) for i in range(2)]
        bank_ctx = ctx.enter_context(nc.psum_tensor("bank_ctx", [P, TOK], F32))
        bank_sum = ctx.enter_context(nc.psum_tensor("bank_sum", [P, TOK], F32))

        bias_in = [sem(f"bias_in{i}") for i in range(R)]
        pen_in = [sem(f"pen_in{i}") for i in range(R)]
        k_in = sem("k_in")
        q_in = [sem(f"q_in{i}") for i in range(2)]
        v_in = [sem(f"v_in{i}") for i in range(2)]
        masked = sem("masked")
        scored = sem("scored")
        added = sem("added")
        max_ready = sem("max_ready")
        exp_done = sem("exp_done")
        turned = sem("turned")
        out_act = sem("out_act")
        out_dve = sem("out_dve")
        pv_done = sem("pv_done")
        ctx_copied = sem("ctx_copied")
        ctx_summed = sem("ctx_summed")
        recip_ready = sem("recip_ready")
        ctx_normed = sem("ctx_normed")
        ctx_stored = [sem(f"ctx_stored{i}") for i in range(2)]
        SCORED0, TURNED0, PV0 = 2 * R * CH, 4 * R, 2

        block = ctx.enter_context(nc.Block())

        @block.sync
        def _(sp):
            def load_head(b, pair, h, first):
                it = (b * (GROUPS // B) + pair) * H + h
                for j in range(R):
                    i, hh, qt = it * R + j, j // QT, j % QT
                    sp.wait_ge(turned, i * 4 + 4)
                    sp.dma_start(ring[:, j, :], side[bass.ds(b * H + h, 1), bass.ds((pair * R + j) * P, P), :].rearrange("o q k -> (o q) k")).then_inc(bias_in[j], 16)
                    if first:
                        sp.dma_start(penb[:, j, :], pen_scratch[bass.ds(b * NS + pair * 2 + hh, 1), :, qt * S:(qt + 1) * S].rearrange("o p n -> (o p) n")).then_inc(pen_in[j], 16)
                    if j == 0:
                        sp.wait_ge(scored, it * R * CH + R * CH)
                        for n, part in enumerate((0, 1, 1, 0)):
                            sp.dma_start(keys[DH * n:DH * (n + 1), bass.ds(it % 2, 1), :].rearrange("p o n -> p (o n)").bitcast(F32),
                                         k_parts[bass.ds(b * 2 + part, 1), bass.ds(h * DH, DH), :].rearrange("o d n -> (o d) n")).then_inc(k_in, 16)
                    if qt == 2:
                        sp.wait_ge(scored, it * R * CH + (R + QT * (1 + hh)) * CH)
                        for n, part in enumerate((0, 1, 0, 1)):
                            sp.dma_start(queries[DH * n:DH * (n + 1), hh, :].bitcast(F32),
                                         q_parts[bass.ds(b * 2 + part, 1), bass.ds(h * DH, DH), bass.ds((pair * 2 + hh) * TOK, TOK)].rearrange("o d n -> (o d) n")).then_inc(q_in[hh], 16)

            with sp.Fori(0, B) as b:
                with sp.Fori(0, GROUPS // B) as pair:
                    load_head(b, pair, 0, True)
                    with sp.Fori(1, H) as h:
                        load_head(b, pair, h, False)
            for i in range(2):
                sp.wait_ge(ctx_stored[i], 16 + TRIPS * 16)

        @block.gpsimd
        def _(pool):
            with pool.Fori(0, GROUPS) as g:
                with pool.Fori(0, H) as h:
                    for j in range(R):
                        pool.wait_ge(bias_in[j], (g * H + h) * 16 + 16)
                        pool.wait_ge(pen_in[j], g * 16 + 16)
                        nc.gpsimd.tensor_tensor(ring[:, j, :], ring[:, j, :], penb[:, j, :], ALU.add).then_inc(masked, 1)

        def known(v):
            return isinstance(v, int)

        def live(number, count):
            return not known(number) or 0 <= number < count

        def need(eng, s, v):
            if not known(v) or v > 0:
                eng.wait_ge(s, v)

        def trips(eng, step):
            for j in range(R):
                step(0, j)
            with eng.Fori(1, TRIPS) as it:
                for j in range(R):
                    step(it, j)
            for j in range(R):
                step(TRIPS, j)

        def closing(it, j):
            return it * 2 - 2 if j < QT else it * 2 - 1

        @block.vector
        def _(dve):
            dve.sem_inc(ctx_normed, 1)

            def copy_quarter(it, j, n):
                t, k = it * R + j - 2, (j - 2) % R
                hh, q = k // QT, k % QT
                if live(t, NT):
                    dve.wait_ge(turned, TURNED0 + t * 4 + n + 1)
                    if q == 0 and n == 2:
                        dve.wait_ge(pv_done, PV0 - 1 + (it * 2 if j == 2 else it * 2 + 1))
                    nc.vector.tensor_copy(probT[:, hh, QR * n:QR * (n + 1), q * P:(q + 1) * P],
                                          bankT[n - 2][:].rearrange("p (c q) -> p c q", c=QR)).then_inc(out_dve, 1)

            def add(it, j, c):
                i = it * R + j
                if live(i, NT):
                    dve.wait_ge(scored, SCORED0 + i * CH + c + 1)
                    if c == 0:
                        dve.wait_ge(masked, i + 1)
                    else:
                        dve.wait_ge(added, i * CH + c)
                    dve.nop(nofuse=True)
                    at = ring[:, j, c * CW:(c + 1) * CW]
                    nc.vector.tensor_tensor_reduce(out=at, in0=scores[c][:], in1=at, scale=1.0,
                                                   scalar=max_part[:, j, c - 1:c] if c else MASKED,
                                                   op0=ALU.add, op1=ALU.max,
                                                   accum_out=max_part[:, j, c:c + 1]).then_inc(added, 1)

            def step(it, j):
                i = it * R + j
                unit, hh = closing(it, j) + 1, 1 if j < QT else 0
                dividing = j % QT == 1 and live(unit, UNITS)
                add(it, j, 0)
                if dividing:
                    nc.vector.tensor_scalar(all_masked[:], neg_max[:, hh * QT:(hh + 1) * QT], 4.0, 0.0, ALU.mult, ALU.mult).then_inc(recip_ready, 1)
                add(it, j, 1)
                if dividing:
                    dve.wait_ge(exp_done, i - 1)
                    dve.wait_ge(recip_ready, unit * 3 + 1)
                    nc.vector.tensor_tensor(total[:], sums[:, hh * QT:(hh + 1) * QT], all_masked[:], ALU.add).then_inc(recip_ready, 1)
                if live(i, NT):
                    dve.wait_ge(added, i * CH + CH)
                    nc.vector.tensor_scalar(neg_max[:, j:j + 1], max_part[:, j, CH - 1:CH], -1.0, None, ALU.mult).then_inc(max_ready, 1)
                copy_quarter(it, j, 2)
                if dividing:
                    dve.wait_ge(recip_ready, unit * 3 + 2)
                    nc.vector.reciprocal(recip[:, hh, :], total[:]).then_inc(recip_ready, 1)
                copy_quarter(it, j, 3)
                if j % QT == 2:
                    unit, hh = closing(it, j), 0 if j < QT else 1
                    if live(unit, UNITS):
                        dve.wait_ge(ctx_summed, unit + 2)
                        dve.wait_ge(recip_ready, unit * 3 + 3)
                        dve.wait_ge(ctx_stored[hh], it * 16)
                        nc.vector.tensor_tensor(ctx_out[:, hh, :, :], bank_sum[:, 0:P].rearrange("p (t d) -> p t d", t=QT),
                                                recip[:, hh, :].rearrange("p (t o) -> p t o", o=1).to_broadcast([P, QT, DH]),
                                                ALU.mult).then_inc(ctx_normed, 1)

            trips(dve, step)

        @block.scalar
        def _(act):
            def load_values(it, hh):
                batch, h = it // (TRIPS // B), it % H
                act.dma_start(values[:, hh, :, :].rearrange("p k d -> p (k d)"),
                              v_heads[bass.ds(batch * H + h, 1)].rearrange("o p n -> (o p) n")).then_inc(v_in[hh], 16)

            act.sem_inc(ctx_stored[0], 16)
            act.sem_inc(ctx_stored[1], 16)
            load_values(0, 0)
            load_values(0, 1)

            def step(it, j):
                i = it * R + j
                if live(i - 1, NT):
                    k = (j - 1) % R
                    act.wait_ge(max_ready, i)
                    nc.scalar.activation(ring[:, k, :], ring[:, k, :], ACT.Exp, bias=neg_max[:, k:k + 1],
                                         accum_out=sums[:, k:k + 1]).then_inc(exp_done, 1)
                if live(i - 2, NT):
                    hh, q = ((j - 2) % R) // QT, (j - 2) % QT
                    for n in (0, 1):
                        act.wait_ge(turned, TURNED0 + (i - 2) * 4 + n + 1)
                        if q == 0 and n == 0:
                            act.wait_ge(pv_done, PV0 - 1 + (it * 2 if j == 2 else it * 2 + 1))
                        nc.scalar.copy(probT[:, hh, QR * n:QR * (n + 1), q * P:(q + 1) * P],
                                       bankT[n][:].rearrange("p (c q) -> p c q", c=QR)).then_inc(out_act, 1)
                if j % QT == 1:
                    unit = closing(it, j)
                    if live(unit, UNITS):
                        act.wait_ge(pv_done, PV0 + unit + 1)
                        act.wait_ge(ctx_summed, unit + 1)
                        nc.scalar.copy(ctxp[:], bank_ctx[:]).then_inc(ctx_copied, 1)
                        if not known(it) or it < TRIPS:
                            load_values(it, 0 if j < QT else 1)
                if j % QT == 3:
                    unit, hh = closing(it, j), 0 if j < QT else 1
                    if live(unit, UNITS):
                        trip = it - 1
                        act.wait_ge(ctx_normed, unit + 2)
                        act.dma_start(ctx_scratch[bass.ds((trip // H) * 2 * H + hh * H + trip % H, 1)].rearrange("o p n -> (o p) n"),
                                      ctx_out[:, hh, :, :].rearrange("p t d -> p (t d)")).then_inc(ctx_stored[hh], 16)

            trips(act, step)

        @block.tensor
        def _(pe):
            pe.sem_inc(scored, SCORED0)
            pe.sem_inc(turned, TURNED0)
            pe.sem_inc(pv_done, PV0)
            pe.sem_inc(ctx_summed, 1)

            def score(it, j, c):
                i, hh, q = it * R + j, j // QT, j % QT
                if live(i, NT):
                    if j == 0 and c == 0:
                        pe.wait_ge(k_in, it * 64 + 64)
                    if q == 0 and c == 0:
                        pe.wait_ge(q_in[hh], it * 64 + 64)
                    need(pe, added, i * CH + c - 1)
                    for n in range(CW // N):
                        last = nc.tensor.matmul(scores[c][:, n * N:(n + 1) * N], queries[:, hh, q * P:(q + 1) * P],
                                                keys[:, bass.ds(it % 2, 1), c * CW + n * N:c * CW + (n + 1) * N].rearrange("p o n -> p (o n)"),
                                                start=True, stop=True)
                    last.then_inc(scored, 1)

            def turn(it, j, n):
                t, slot = it * R + j - 2, (j - 2) % R
                if live(t, NT):
                    if n == 0:
                        pe.wait_ge(exp_done, t + 1)
                    if n < 2:
                        need(pe, out_dve, t * 2 - 1 + n)
                    else:
                        pe.wait_ge(out_act, t * 2 - 1 + n)
                    for c in range(QR):
                        at = (QR * n + c) * P
                        last = nc.tensor.transpose(bankT[n % 2][:, c * P:(c + 1) * P], ring[:, slot, at:at + P], ident[:])
                    last.then_inc(turned, 1)

            def weigh(it, j):
                n = (j - 2) % QT
                unit = it * 2 - 2 if j < 2 else it * 2 - 1 if j < 6 else it * 2
                hh = 1 if 2 <= j < 6 else 0
                if live(unit, UNITS):
                    if n == 0:
                        pe.wait_ge(v_in[hh], it * 16 if j == 2 else it * 16 + 16)
                        need(pe, ctx_copied, unit)
                    pe.wait_ge(out_act if n < 2 else out_dve, (unit * QT + QT - 1) * 2 + n % 2 + 1)
                    for c in range(4):
                        last = nc.tensor.matmul(bank_ctx[DH * c:DH * (c + 1), :], values[:, hh, QR * n + c, :],
                                                probT[:, hh, QR * n + c, :], start=(n == 0), stop=(n == 3))
                    if n == 3:
                        last.then_inc(pv_done, 1)

            def close(it, j):
                unit = closing(it, j)
                if live(unit, UNITS):
                    pe.wait_ge(ctx_copied, unit + 1)
                    pe.wait_ge(ctx_normed, unit + 1)
                    for t in range(QT):
                        last = nc.tensor.matmul(bank_sum[:, t * DH:(t + 1) * DH], ctxp[:, t * P:(t + 1) * P], sel4[:],
                                                start=True, stop=True)
                    last.then_inc(ctx_summed, 1)

            def step(it, j):
                score(it, j, 0)
                score(it, j, 1)
                turn(it, j, 0)
                turn(it, j, 1)
                if j % QT == 2:
                    close(it, j)
                weigh(it, j)
                turn(it, j, 2)
                turn(it, j, 3)

            trips(pe, step)


def phase_c(nc, sem, ctx_scratch, xm_scratch, Wo, bo, W1, b1, W2, b2, g2, beta2, out, ident, trig):
    with ExitStack() as ctx:
        def sb(name, shape, dt=F32):
            return ctx.enter_context(nc.sbuf_tensor(name, shape, dt))

        wo = sb("wo", [P, DB, D])
        w1 = sb("w1", [P, DB, F])
        w2 = sb("w2", [P, FB, D])
        b1_col = sb("b1_col", [P, FB])
        b1_scaled = sb("b1_scaled", [P, FB])
        bo_all, b2_all, g2_all, beta2_all = (sb(n, [P, D]) for n in ("bo_all", "b2_all", "g2_all", "beta2_all"))
        eps_c = sb("eps_c", [P, 1])
        cosines = sb("cosines", [P, B, 2])
        sines = sb("sines", [P, B, 2])
        ctx_in = sb("ctx_in", [P, QT, H, DH])
        xm_in = sb("xm_in", [P, QT, D])
        ctxT = sb("ctxT", [P, DB, TOK])
        x2 = sb("x2", [P, 2, QT, D])
        stats = sb("stats_c", [P, QT, 6])
        mean_var = sb("mean_var_c", [P, QT, 2])
        std = sb("std_c", [P, QT])
        rstd = sb("rstd_c", [P, QT])
        hn = sb("hn", [P, QT, D])
        hT = sb("hT", [P, 2, DB, TOK])
        gate = sb("gate", [P, 2, TOK])
        hidden = sb("hidden", [P, 4, TOK])
        y = sb("y", [P, QT, D])
        rot_a = sb("rot_a", [P, 2, D])
        rot_b = sb("rot_b", [P, 2, D])
        y_out = sb("y_out", [P, 2, D])
        acc = [ctx.enter_context(nc.psum_tensor(f"c_acc{i}", [P, D], F32)) for i in range(QT)]
        up = [ctx.enter_context(nc.psum_tensor(f"c_up{i}", [P, TOK], F32)) for i in range(2)]
        fore = [ctx.enter_context(nc.psum_tensor(f"c_fore{i}", [P, TOK], F32)) for i in range(2)]

        vec_in = sem("vec_in")
        wo_in, w1_in, w2_in = sem("wo_in"), sem("w1_in"), sem("w2_in")
        consts_ready = sem("consts_ready")
        ctx_ld, xm_ld = sem("ctx_ld"), sem("xm_ld")
        ctx_turned = sem("ctx_turned")
        ctxT_ready = sem("ctxT_ready")
        wo_done = sem("wo_done")
        x2_ready = sem("x2_ready")
        c_chain = sem("c_chain")
        c_var, c_std = sem("c_var"), sem("c_std")
        hn_ready = sem("hn_ready")
        h_turned = sem("h_turned")
        hT_ready = sem("hT_ready")
        up_done = sem("up_done")
        gate_ready = sem("gate_ready")
        hid_ready = sem("hid_ready")
        down_done = sem("down_done")
        acc_read = sem("acc_read")
        rotated = sem("rotated")
        y_ready = sem("y_ready")
        y_stored = [sem(f"y_stored{i}") for i in range(2)]      

        block = ctx.enter_context(nc.Block())

        def need(eng, s, v):
            if not isinstance(v, int) or v > 0:
                eng.wait_ge(s, v)

        def of(buffer, u):
            return buffer[:, bass.ds(u % 2, 1)].rearrange("p o t n -> p (o t) n")

        def supertiles(eng, ffn, front):
            for f in range(FB):
                front(0, f)
            with eng.Fori(0, NU - 1) as u:
                for f in range(FB + 2):
                    ffn(u, f)
                    if f < FB:
                        front(u + 1, f)
            for f in range(FB + 2):
                ffn(NU - 1, f)

        @block.sync
        def _(sp):
            def row(v):
                return v.rearrange("(o n) -> o n", o=1).to_broadcast([P, D])

            def load(v):
                need(sp, ctx_turned, v * DB)
                for t in range(QT):
                    sp.dma_start(ctx_in[:, t, :, :],
                                 ctx_scratch[bass.ds(v * H, H), :, t * DH:(t + 1) * DH].rearrange("h p d -> p h d")).then_inc(ctx_ld, 16)
                need(sp, x2_ready, v * QT)
                sp.dma_start(xm_in[:].rearrange("p t n -> p (t n)"),
                             xm_scratch[bass.ds(v, 1)].rearrange("o p n -> (o p) n")).then_inc(xm_ld, 16)

            sp.dma_start(wo[:], Wo.rearrange("(c p) n -> p c n", p=P)).then_inc(wo_in, 16)
            load(0)
            for to, v in ((bo_all, bo), (b2_all, b2), (g2_all, g2), (beta2_all, beta2)):
                sp.dma_start(to[:], row(v)).then_inc(vec_in, 16)
            sp.dma_start(b1_col[:], b1.rearrange("(c p) -> p c", p=P), allow_slow_non_contiguous=True).then_inc(vec_in, 16)
            with sp.Fori(1, NU) as v:
                load(v)

        @block.gpsimd
        def _(pool):
            pool.wait_ge(xm_ld, 16)
            for c in range(4):
                pool.dma_start(w1[:, :, c * D:(c + 1) * D], W1.rearrange("(c p) n -> p c n", p=P)[:, :, c * D:(c + 1) * D]).then_inc(w1_in, 16)
            for c in range(4):
                pool.dma_start(w2[:, 4 * c:4 * c + 4, :], W2.rearrange("(c p) n -> p c n", p=P)[:, 4 * c:4 * c + 4, :]).then_inc(w2_in, 16)
            pool.sem_inc(y_ready, 2)

            def finish(u):
                for t in range(QT):
                    pool.wait_ge(rotated, u * QT + t + 1)
                    need(pool, y_stored[t % 2], u * 32 + (t // 2) * 16)
                    nc.gpsimd.tensor_tensor(y_out[:, t % 2, :], rot_a[:, t % 2, :], rot_b[:, t % 2, :], ALU.add).then_inc(y_ready, 1)
                    pool.wait_ge(y_ready, u * QT + t + 3)
                    pool.dma_start(out[bass.ds(u, 1), t * P:(t + 1) * P, :].rearrange("o p n -> (o p) n"),
                                   y_out[:, t % 2, :]).then_inc(y_stored[t % 2], 16)

            finish(0)
            with pool.Fori(1, NU) as u:
                finish(u)
            for i in range(2):
                pool.wait_ge(y_stored[i], NU * QT // 2 * 16)

        @block.scalar
        def _(act):
            def front(v, f):
                if f < DB:
                    act.wait_ge(ctx_turned, v * DB + f + 1)
                    if f == 0:
                        need(act, wo_done, v * QT)
                    nc.scalar.copy(ctxT[:, f, :], fore[f % 2][:]).then_inc(ctxT_ready, 1)
                if f == 9:
                    act.wait_ge(c_var, v + 1)
                    nc.scalar.activation(std[:], mean_var[:, :, 1], ACT.Sqrt, bias=eps_c[:]).then_inc(c_std, 1)
                if f >= FB - DB:
                    c = f - (FB - DB)
                    act.wait_ge(h_turned, v * DB + c + 1)
                    nc.scalar.copy(hT[:, bass.ds(v % 2, 1), c, :].rearrange("p o n -> p (o n)"), fore[c % 2][:]).then_inc(hT_ready, 1)

            def ffn(u, f):
                if f < FB:
                    act.wait_ge(up_done, u * FB + f + 1)
                    act.wait_ge(hid_ready, u * FB + f + 3)
                    nc.scalar.activation(gate[:, f % 2, :], up[f % 2][:], ACT.Sigmoid, scale=1.702,
                                         bias=b1_scaled[:, f:f + 1]).then_inc(gate_ready, 1)

            act.wait_ge(consts_ready, 1)
            supertiles(act, ffn, front)

        @block.vector
        def _(dve):
            LINKS = 6

            def front(v, f):
                def link(ins, n):
                    ins.then_inc(c_chain, 1)
                    dve.wait_ge(c_chain, v * LINKS + n)

                x2_v = of(x2, v)
                if f == 0:
                    dve.wait_ge(xm_ld, v * 16 + 16)
                    for t in range(QT):
                        last = nc.vector.tensor_tensor(xm_in[:, t, :], xm_in[:, t, :], bo_all[:], ALU.add)
                    link(last, 1)
                if 4 <= f < 8:
                    t = f - 4
                    dve.wait_ge(wo_done, v * QT + t + 1)
                    nc.vector.tensor_tensor(x2_v[:, t, :], fore[t % 2][:], xm_in[:, t, :], ALU.add).then_inc(x2_ready, 1)
                if f == 8:
                    dve.wait_ge(x2_ready, v * QT + QT)
                    dve.nop(nofuse=True)
                    for t in range(QT):
                        last = nc.vector.bn_stats(stats[:, t, :], x2_v[:, t, :])
                    link(last, 2)
                    dve.nop(nofuse=True)
                    for t in range(QT):
                        last = nc.vector.bn_aggr(mean_var[:, t, :], stats[:, t, :])
                    last.then_inc(c_var, 1)
                if f == 9:
                    dve.wait_ge(c_std, v + 1)
                    link(nc.vector.reciprocal(rstd[:], std[:]), 3)
                    need(dve, h_turned, v * DB)
                    for t in range(QT):
                        last = nc.vector.tensor_scalar(hn[:, t, :], x2_v[:, t, :], mean_var[:, t, 0:1], rstd[:, t:t + 1], ALU.subtract, ALU.mult)
                    link(last, 4)
                if f == 10:
                    for t in range(QT):
                        last = nc.vector.tensor_tensor(hn[:, t, :], hn[:, t, :], g2_all[:], ALU.mult)
                    link(last, 5)
                    for t in range(QT):
                        last = nc.vector.tensor_tensor(hn[:, t, :], hn[:, t, :], beta2_all[:], ALU.add)
                    last.then_inc(hn_ready, 1)
                if f == 11:
                    for t in range(QT):
                        last = nc.vector.tensor_tensor(x2_v[:, t, :], x2_v[:, t, :], b2_all[:], ALU.add)
                    link(last, LINKS)

            def ffn(u, f):
                if f < FB:
                    dve.wait_ge(gate_ready, u * FB + f + 1)
                    dve.wait_ge(down_done, u * FB + f + 1)
                    nc.vector.scalar_tensor_tensor(out=hidden[:, f % 4, :], in0=up[f % 2][:], scalar=b1_col[:, f:f + 1],
                                                   in1=gate[:, f % 2, :], op0=ALU.add, op1=ALU.mult).then_inc(hid_ready, 1)
                if f == FB + 1:
                    dve.wait_ge(down_done, u * FB + FB + 4)
                    for t in range(QT):
                        nc.vector.tensor_tensor(y[:, t, :], acc[t][:], of(x2, u)[:, t, :], ALU.add).then_inc(acc_read, 1)
                    for t in range(QT):
                        dve.wait_ge(acc_read, u * QT + t + 5)
                        dve.wait_ge(y_ready, u * QT + t + 1)
                        pairs = y[:, t, :].rearrange("p (n k e) -> p n k e", k=2, e=2)
                        to_a = rot_a[:, t % 2, :].rearrange("p (n k e) -> p n k e", k=2, e=2)
                        to_b = rot_b[:, t % 2, :].rearrange("p (n k e) -> p n k e", k=2, e=2)
                        for k in range(2):
                            cos_k = cosines[:, bass.ds(u // NS, 1), k:k + 1].rearrange("p o n -> p (o n)")
                            sin_k = sines[:, bass.ds(u // NS, 1), k:k + 1].rearrange("p o n -> p (o n)")
                            nc.vector.tensor_scalar(to_a[:, :, k, :], pairs[:, :, k, :], cos_k, None, ALU.mult)
                            nc.vector.tensor_scalar(to_b[:, :, k, 0], pairs[:, :, k, 1], sin_k, None, ALU.mult)
                            last = nc.vector.tensor_scalar(to_b[:, :, k, 1], pairs[:, :, k, 0], sin_k, -1.0, ALU.mult, ALU.mult)
                        last.then_inc(rotated, 1)

            nc.vector.memset(eps_c[:], EPS)
            for b in range(B):
                for k in range(2):
                    nc.vector.tensor_copy(sines[:, b, k:k + 1], trig[:, 8 + 2 * k + b:9 + 2 * k + b])
                    nc.vector.tensor_copy(cosines[:, b, k:k + 1], trig[:, 12 + 2 * k + b:13 + 2 * k + b])
            dve.wait_ge(vec_in, 80)
            nc.vector.tensor_scalar(b1_scaled[:], b1_col[:], 1.702, None, ALU.mult).then_inc(consts_ready, 1)
            dve.wait_ge(consts_ready, 1)
            dve.sem_inc(hid_ready, 4)
            dve.sem_inc(acc_read, 4)
            supertiles(dve, ffn, front)

        @block.tensor
        def _(pe):
            def front(v, f):
                if f < DB:
                    if f == 0:
                        pe.wait_ge(ctx_ld, v * 64 + 64)
                    if f < 2:
                        need(pe, hT_ready, v * DB - 1 + f)
                    else:
                        pe.wait_ge(ctxT_ready, v * DB + f - 1)
                    for t in range(QT):
                        last = nc.tensor.transpose(fore[f % 2][:, t * P:(t + 1) * P], ctx_in[:, t, 4 * f:4 * f + 4, :].rearrange("p h d -> p (h d)"), ident[:])
                    last.then_inc(ctx_turned, 1)
                elif f < 8:
                    t = f - 4
                    if t < 2:
                        pe.wait_ge(ctxT_ready, v * DB + DB)
                    else:
                        pe.wait_ge(x2_ready, v * QT + t - 1)
                    for c in range(DB):
                        last = nc.tensor.matmul(fore[t % 2][:], ctxT[:, c, t * P:(t + 1) * P], wo[:, c, :], start=(c == 0), stop=(c == DB - 1))
                    last.then_inc(wo_done, 1)
                elif f >= FB - DB:
                    c = f - (FB - DB)
                    if c == 0:
                        pe.wait_ge(hn_ready, v + 1)
                    if c >= 2:
                        pe.wait_ge(hT_ready, v * DB + c - 1)
                    for t in range(QT):
                        last = nc.tensor.transpose(fore[c % 2][:, t * P:(t + 1) * P], hn[:, t, c * P:(c + 1) * P], ident[:])
                    last.then_inc(h_turned, 1)

            def ffn(u, f):
                if f == 0:
                    pe.wait_ge(hT_ready, u * DB + DB)
                    pe.wait_ge(w1_in, 64)
                if f < FB:
                    pe.wait_ge(hid_ready, u * FB + f + 3)
                    for c in range(DB):
                        last = nc.tensor.matmul(up[f % 2][:], w1[:, c, f * P:(f + 1) * P], hT[:, bass.ds(u % 2, 1), c, :].rearrange("p o n -> p (o n)"),
                                                start=(c == 0), stop=(c == DB - 1))
                    last.then_inc(up_done, 1)
                if f >= 2:
                    k = f - 2
                    pe.wait_ge(hid_ready, u * FB + k + 5)
                    if k == 0:
                        pe.wait_ge(w2_in, 64)
                        pe.wait_ge(acc_read, u * QT + 4)
                    for t in range(QT):
                        last = nc.tensor.matmul(acc[t][:], hidden[:, k % 4, t * P:(t + 1) * P], w2[:, k, :], start=(k == 0), stop=(k == FB - 1))
                    last.then_inc(down_done, 1)

            pe.sem_inc(down_done, 4)
            pe.wait_ge(wo_in, 16)
            supertiles(pe, ffn, front)


def build(nc, a, out):
    q_parts = nc.dram_tensor("q_parts", (B * 2, D, S), F32, kind="Internal").ap()
    k_parts = nc.dram_tensor("k_parts", (B * 2, D, S), F32, kind="Internal").ap()
    v_heads = nc.dram_tensor("v_heads", (B * H, P, KB * DH), F32, kind="Internal").ap()
    xm_scratch = nc.dram_tensor("xm_scratch", (NU, P, QT * D), F32, kind="Internal").ap()
    pen_scratch = nc.dram_tensor("pen_scratch", (NU, P, QT * S), BF16, kind="Internal").ap()
    ctx_scratch = nc.dram_tensor("ctx_scratch", (NU * H, P, QT * DH), F32, kind="Internal").ap()
    with ExitStack() as ctx:
        def sem(name):
            return ctx.enter_context(nc.semaphore(name))

        ident = ctx.enter_context(nc.sbuf_tensor("ident", [P, P], F32))
        sel4 = ctx.enter_context(nc.sbuf_tensor("sel4", [P, DH], F32))
        trig = ctx.enter_context(nc.sbuf_tensor("trig", [P, 16], F32))
        phase_a(nc, sem, a["x"], a["itok_B_34_63"], a["mask_Bx1xSxS_bk0"], a["condB_theta"], a["condB_phi"],
                a["L0_cond_W_ada"], a["L0_cond_b_ada"], a["L0_cond_Wq"], a["L0_cond_bq"], a["L0_cond_Wk"], a["L0_cond_bk"],
                a["L0_cond_Wv"], a["L0_cond_bv"], a["freqs"], q_parts, k_parts, v_heads, xm_scratch, pen_scratch,
                ident, sel4, trig)
        phase_b(nc, sem, a["fside_Bx16xSxS_0"], q_parts, k_parts, v_heads, pen_scratch, ctx_scratch, ident, sel4)
        phase_c(nc, sem, ctx_scratch, xm_scratch, a["L0_cond_Wo"], a["L0_cond_bo"], a["L0_cond_W1"], a["L0_cond_b1"],
                a["L0_cond_W2"], a["L0_cond_b2"], a["L0_cond_g2"], a["L0_cond_beta2"], out, ident, trig)


_VECTORS = ["itok_B_34_63", "condB_theta", "condB_phi"] + ["L0_cond_" + n for n in
            ("W_ada", "b_ada", "Wq", "bq", "Wk", "bk", "Wv", "bv", "Wo", "bo", "W1", "b1", "W2", "b2", "g2", "beta2")]


def kernel(**inputs):
    import numpy as _np
    import concourse.bacc as _bacc
    from concourse import mybir as _mybir
    from concourse.bass_utils import run_bass_kernel_spmd as _run

    nc = _bacc.Bacc("TRN2", target_bir_lowering=False, num_devices=1)
    arrays = {n: _np.ascontiguousarray(inputs[n]) for n in _VECTORS}
    arrays["x"] = _np.ascontiguousarray(inputs["x"]).reshape(NU, TOK, D)
    arrays["fside_Bx16xSxS_0"] = _np.ascontiguousarray(inputs["fside_Bx16xSxS_0"]).reshape(B * H, S, S)
    arrays["mask_Bx1xSxS_bk0"] = _np.ascontiguousarray(inputs["mask_Bx1xSxS_bk0"]).reshape(NU, TOK, S)
    half = D // 2
    arrays["freqs"] = _np.exp(_np.arange(half, dtype=_np.float32) * _np.float32(-math.log(10000.0) / (half - 1)))
    aps = {n: nc.dram_tensor(f"in_{n}", v.shape, _mybir.dt.from_np(v.dtype), kind="ExternalInput").ap() for n, v in arrays.items()}
    out = nc.dram_tensor("out_0", (NU, TOK, D), _mybir.dt.float32, kind="ExternalOutput").ap()
    build(nc, aps, out)
    r = _run(nc, [{f"in_{n}": v for n, v in arrays.items()}], core_ids=[0])
    return r.results[0]["out_0"].reshape(B, S, D)
```
